# Optimizing a Trainium2 kernel written in Bass

```python
import numpy as np
import jax
import jax.numpy as jnp

def _softmax(x, axis=-1):
    return jax.nn.softmax(x, axis=axis)

def _gelu(x):
    return jax.nn.gelu(x, approximate=True)

def _silu(x):
    return jax.nn.silu(x)

def _sigmoid(x):
    return jax.nn.sigmoid(x)

def _layernorm(x, axis=-1, eps=1e-05):
    m = jnp.mean(x, axis=axis, keepdims=True)
    v = jnp.var(x, axis=axis, keepdims=True)
    return (x - m) / jnp.sqrt(v + eps)

def _scatter_add(tgt, idx, src, axis=0):
    return tgt.at[idx].add(src)

def _segment_sum(src, seg, n):
    return jax.ops.segment_sum(src, seg, n)
kernel_name = 'mk_adaln_d1_jaxref_r8_91eace'

def setup_inputs(seed: int=0):
    np.random.seed(seed)
    _w = jnp.asarray

    def _L0_attn_setup():
        import jax, jax.numpy as jnp
        import numpy as np
        EPS = 1e-06
        N_HEADS = 16

        def _project_static(x):
            sp = jnp.clip(x[..., 1:], -8.0, 8.0)
            x0 = jnp.sqrt(1.0 + jnp.sum(sp * sp, axis=-1, keepdims=True) + EPS)
            return jnp.concatenate([x0, sp], axis=-1)

        def _inner_static(x, y):
            return -x[..., 0] * y[..., 0] + jnp.sum(x[..., 1:] * y[..., 1:], axis=-1)

        def _log_map_approx(x, y):
            y = _project_static(y)
            xy = _inner_static(x, y)
            xy = jnp.minimum(xy, -(1.0 + EPS))[..., None]
            d = jnp.maximum(jnp.arccosh(jnp.maximum(-xy, 1.0 + EPS)), 0.001)
            dirv = y + xy * x
            dn = jnp.sqrt(jnp.maximum(_inner_static(dirv, dirv), EPS))[..., None]
            return d * dirv / (dn + EPS)

        def _dynamic_metric(x, mu, W1, b1, W2, b2):
            d = x.shape[-1]
            eta = jnp.ones((d,), x.dtype).at[0].set(-1.0)
            v = x - mu
            h = jnp.tanh(jnp.tanh(v @ W1.T + b1) @ W2.T + b2) * 0.1
            g = eta + h
            return jnp.concatenate([-jnp.abs(g[..., :1]), jnp.abs(g[..., 1:])], axis=-1)
        key = jax.random.key(seed)
        ks = jax.random.split(key, 9)
        B, T, d = (2, 256, 128)
        s = 0.02
        return {'x': jax.random.normal(ks[0], (B, T, d), jnp.float32), 'W1': jax.random.normal(ks[1], (2 * d, d), jnp.float32) * s, 'b1': jax.random.normal(ks[2], (2 * d,), jnp.float32) * s, 'W2': jax.random.normal(ks[3], (d, 2 * d), jnp.float32) * s, 'b2': jax.random.normal(ks[4], (d,), jnp.float32) * s, 'Wq': jax.random.normal(ks[5], (d, d), jnp.float32) * s, 'Wk': jax.random.normal(ks[6], (d, d), jnp.float32) * s, 'Wv': jax.random.normal(ks[7], (d, d), jnp.float32) * s, 'Wo': jax.random.normal(ks[8], (d, d), jnp.float32) * s}
    _L0_attn_in = _L0_attn_setup()

    def _L0_ffn_setup():
        import jax, jax.numpy as jnp
        import numpy as np
        DIM = 128
        HIDDEN = 384
        SCALE = 1.0 / 127.0

        def _dequant(w_int, dtype):
            return w_int.astype(dtype) * jnp.asarray(SCALE, dtype)
        key = jax.random.key(seed)
        k_x, k_g, k_u, k_d = jax.random.split(key, 4)
        x = jax.random.normal(k_x, (4, 256, DIM), dtype=jnp.float32)
        w_gate = jax.random.randint(k_g, (HIDDEN, DIM), -127, 128, dtype=jnp.int32)
        w_up = jax.random.randint(k_u, (HIDDEN, DIM), -127, 128, dtype=jnp.int32)
        w_down = jax.random.randint(k_d, (DIM, HIDDEN), -127, 128, dtype=jnp.int32)
        return {'x': x, 'w_gate': w_gate, 'w_up': w_up, 'w_down': w_down}
    _L0_ffn_in = _L0_ffn_setup()
    _L0_c = _w((lambda *s: np.random.randn(*s).astype(np.float32) * 0.05)(1, 128))
    _L0_wmod = _w((lambda *s: np.random.randn(*s).astype(np.float32) * 0.05)(128, 6 * 128) * 128 ** (-0.5))
    _d = {'L0_attn_x': _L0_attn_in['x'], 'L0_attn_W1': _L0_attn_in['W1'], 'L0_attn_b1': _L0_attn_in['b1'], 'L0_attn_W2': _L0_attn_in['W2'], 'L0_attn_b2': _L0_attn_in['b2'], 'L0_attn_Wq': _L0_attn_in['Wq'], 'L0_attn_Wk': _L0_attn_in['Wk'], 'L0_attn_Wv': _L0_attn_in['Wv'], 'L0_attn_Wo': _L0_attn_in['Wo'], 'L0_ffn_w_gate': _L0_ffn_in['w_gate'], 'L0_ffn_w_up': _L0_ffn_in['w_up'], 'L0_ffn_w_down': _L0_ffn_in['w_down'], 'L0_c': _L0_c, 'L0_wmod': _L0_wmod}
    _x0 = _d['L0_attn_x']
    _d['L0_attn_x'] = jax.random.normal(jax.random.fold_in(jax.random.key(seed), 1), (1, 2048, 128), dtype=_x0.dtype)
    del _x0
    return _d

def reference(L0_attn_x, L0_attn_W1, L0_attn_b1, L0_attn_W2, L0_attn_b2, L0_attn_Wq, L0_attn_Wk, L0_attn_Wv, L0_attn_Wo, L0_ffn_w_gate, L0_ffn_w_up, L0_ffn_w_down, L0_c, L0_wmod):

    def _L0_attn_ref(x, W1, b1, W2, b2, Wq, Wk, Wv, Wo):
        import jax, jax.numpy as jnp
        import numpy as np
        EPS = 1e-06
        N_HEADS = 16

        def _project_static(x):
            sp = jnp.clip(x[..., 1:], -8.0, 8.0)
            x0 = jnp.sqrt(1.0 + jnp.sum(sp * sp, axis=-1, keepdims=True) + EPS)
            return jnp.concatenate([x0, sp], axis=-1)

        def _inner_static(x, y):
            return -x[..., 0] * y[..., 0] + jnp.sum(x[..., 1:] * y[..., 1:], axis=-1)

        def _log_map_approx(x, y):
            y = _project_static(y)
            xy = _inner_static(x, y)
            xy = jnp.minimum(xy, -(1.0 + EPS))[..., None]
            d = jnp.maximum(jnp.arccosh(jnp.maximum(-xy, 1.0 + EPS)), 0.001)
            dirv = y + xy * x
            dn = jnp.sqrt(jnp.maximum(_inner_static(dirv, dirv), EPS))[..., None]
            return d * dirv / (dn + EPS)

        def _dynamic_metric(x, mu, W1, b1, W2, b2):
            d = x.shape[-1]
            eta = jnp.ones((d,), x.dtype).at[0].set(-1.0)
            v = x - mu
            h = jnp.tanh(jnp.tanh(v @ W1.T + b1) @ W2.T + b2) * 0.1
            g = eta + h
            return jnp.concatenate([-jnp.abs(g[..., :1]), jnp.abs(g[..., 1:])], axis=-1)
        B, T, d = x.shape
        h, dh = (N_HEADS, d // N_HEADS)
        mu = jnp.zeros((d,), x.dtype).at[0].set(1.0)
        mu = jnp.broadcast_to(mu, (B, T, d))
        v = _log_map_approx(mu, x)
        q = (v @ Wq.T).reshape(B, T, h, dh).transpose(0, 2, 1, 3)
        k = (v @ Wk.T).reshape(B, T, h, dh).transpose(0, 2, 1, 3)
        vv = (v @ Wv.T).reshape(B, T, h, dh).transpose(0, 2, 1, 3)
        g_x = _dynamic_metric(x, mu, W1, b1, W2, b2)
        gh = g_x.reshape(B, T, h, dh).transpose(0, 2, 1, 3)
        sc = jnp.einsum('bhqd,bhkd->bhqk', q * gh, k) / jnp.sqrt(jnp.asarray(dh, x.dtype))
        at = jax.nn.softmax(sc, axis=-1)
        out = jnp.einsum('bhqk,bhkd->bhqd', at, vv).transpose(0, 2, 1, 3).reshape(B, T, d)
        out = out @ Wo.T
        return _project_static(_project_static(mu) + out * 0.1)

    def _L0_ffn_ref(x, w_gate, w_up, w_down):
        import jax, jax.numpy as jnp
        import numpy as np
        DIM = 128
        HIDDEN = 384
        SCALE = 1.0 / 127.0

        def _dequant(w_int, dtype):
            return w_int.astype(dtype) * jnp.asarray(SCALE, dtype)
        wg = _dequant(w_gate, x.dtype)
        wu = _dequant(w_up, x.dtype)
        wd = _dequant(w_down, x.dtype)
        gate = jnp.einsum('bsd,hd->bsh', x, wg)
        up = jnp.einsum('bsd,hd->bsh', x, wu)
        h = jax.nn.silu(gate) * up
        return jnp.einsum('bsh,dh->bsd', h, wd)
    x = L0_attn_x
    mod = (_silu(L0_c) @ L0_wmod).reshape(L0_c.shape[0], 6, 1, -1)
    sa, ca, ga, sb, cb, gb = (mod[:, 0], mod[:, 1], mod[:, 2], mod[:, 3], mod[:, 4], mod[:, 5])
    ga = (2 * (ga >= 0) - 1) * jnp.maximum(jnp.abs(ga), 0.25)
    gb = (2 * (gb >= 0) - 1) * jnp.maximum(jnp.abs(gb), 0.25)
    h = _layernorm(x, axis=-1) * (1 + ca) + sa
    x = x + ga * _L0_attn_ref(h, L0_attn_W1, L0_attn_b1, L0_attn_W2, L0_attn_b2, L0_attn_Wq, L0_attn_Wk, L0_attn_Wv, L0_attn_Wo)
    h = _layernorm(x, axis=-1) * (1 + cb) + sb
    x = x + gb * _L0_ffn_ref(h, L0_ffn_w_gate, L0_ffn_w_up, L0_ffn_w_down)
    return x

_drawn_inputs = setup_inputs


def setup_inputs(seed=0):
    import zlib

    import numpy as np

    out = dict(_drawn_inputs(seed))
    spreads = {}
    factors = {'L0_attn_W1': 64.0,
     'L0_attn_b1': 64.0,
     'L0_attn_W2': 64.0,
     'L0_attn_b2': 64.0,
     'L0_attn_Wq': 64.0,
     'L0_attn_Wk': 64.0,
     'L0_attn_Wv': 64.0,
     'L0_attn_Wo': 64.0}
    for name, (base, spread) in spreads.items():
        noise = np.random.default_rng([zlib.crc32(name.encode()), seed]).standard_normal(out[name].shape)
        drawn = base * np.exp(spread * noise) if base else spread * noise
        out[name] = jnp.asarray(drawn.astype(out[name].dtype))
    for name, factor in factors.items():
        out[name] = (out[name] * factor).astype(out[name].dtype)
    return out
```

```python
from contextlib import ExitStack

import numpy as np

import concourse.bass as bass
from concourse import mybir

F32, BF16, I32 = mybir.dt.float32, mybir.dt.bfloat16, mybir.dt.int32
ALU = mybir.AluOpType
ACT = mybir.ActivationFunctionType
AX = mybir.AxisListType

T, D, H = 2048, 128, 16
DH = D // H
P = 128
NT = T // P
BT = 512
NB = T // BT
TPB = BT // P
GH = 4
NG = H // GH
VW = 2 * DH
PARTS = 3
SHIFT_ROW = 96
HID = 384
NM = HID // P
MH = 2 * D // P
STEPS = NG * NT
EPS, LN_EPS = 1e-6, 1e-5
FFN_SCALE = 1.0 / 127.0
HEADROOM = 48.0
ARENA = 41 * 256
SUM_FLOOR = 2.0 ** -86
BIG = 1.0e38

AT_WO, AT_TR, AT_GATE, AT_UP, AT_DOWN = 7, 14, (18, 22, 27), (20, 25, 30), 37
M1_BANK, M2_BANK, NQ_BANK = ((2, 3), (4, 5), (6, 7), (7, 6)), (6, 7, 6, 7), (2, 3, 4, 5)
AT_Q = (4, 12, 20)
ONE_PAIR = float(np.array([0x3F803F80], np.uint32).view(np.float32)[0])


class Chain:

    def __init__(self, eng, sem, start=0):
        self.eng, self.sem, self.start, self.n = eng, sem, start, 0

    def did(self, ins):
        ins.then_inc(self.sem, 1)
        self.n += 1

    def after(self):
        self.eng.wait_ge(self.sem, self.start + self.n)


def build(nc, x, columns, wmod, fixed, w1t, w2t, w_att, wgt, wut, wdt, out):
    with ExitStack() as ctx:
        def sb(name, shape, dt=F32):
            return ctx.enter_context(nc.sbuf_tensor(name, shape, dt))

        def sem(name):
            return ctx.enter_context(nc.semaphore(name))

        q_scr = nc.dram_tensor("q_scr", (PARTS, D, T), BF16, kind="Internal").ap()
        k_scr = nc.dram_tensor("k_scr", (H, PARTS, DH, T), BF16, kind="Internal").ap()
        shift_scr = nc.dram_tensor("shift_scr", (H, PARTS, T), BF16, kind="Internal").ap()

        w1_sb = sb("w1_sb", [P, MH * P])
        w2_sb = sb("w2_sb", [P, MH, D])
        w_att_sb = sb("w_att_sb", [P, 4, D])
        wk_sb, wv_sb, wq_sb, wo_sb = (w_att_sb[:, i, :] for i in range(4))
        wmod_sb = sb("wmod_sb", [P, 6 * D])
        mod = sb("mod", [P, 6 * D])
        fixed_sb = sb("fixed_sb", [P, P + H])
        ident_sb = fixed_sb[:, 0:P]
        hs_sb = fixed_sb[:, P:P + H]
        ones_bf = sb("ones_bf", [P, T], BF16)
        cols = sb("cols", [P, 8])
        b1_c, b2_c, eta_c, mmu_c, c_c, eta_s = cols[:, 0:2], cols[:, 2:3], cols[:, 3:4], cols[:, 4:5], cols[:, 5:6], \
            cols[:, 6:7]
        hs_bf = sb("hs_bf", [P, H], BF16)
        silu_c = sb("silu_c", [P, 2])
        silu_b = sb("silu_b", [P, P])
        half = sb("half", [P, NT])
        mhalf = sb("mhalf", [P, NT])
        wg_f, wu_f = sb("wg_f", [P, HID]), sb("wu_f", [P, HID])
        wd_f = sb("wd_f", [P, NM, D])

        x_tm = sb("x_tm", [P, NT, D])
        K_op = sb("K_op", [P, H, T], BF16)
        Q_op = sb("Q_op", [P, 2 * H * BT], BF16)
        V_op = sb("V_op", [P, NT, H * VW + VW])
        probs = sb("probs", [P, 4, 2 * BT])
        O_sb = sb("O_sb", [P, NG, BT])

        arena = sb("arena", [P, ARENA])
        at = [0]

        def tmp(words, *shape, dt=F32):
            v = arena[:, at[0]:at[0] + words]
            at[0] += words
            assert at[0] <= ARENA
            if dt != F32:
                v = v.bitcast(dt)
            if len(shape) == 2:
                v = v.rearrange("p (a b) -> p a b", a=shape[0])
            return v

        num_T = tmp(BT)
        den_T = tmp(BT)
        over = at[0]
        h_tm = tmp(NT * D, NT, D)
        sp_tm = tmp(NT * D, NT, D)
        g_fm = tmp(NB * BT, NB, BT)
        q_parts = [tmp(PARTS * BT // 2, PARTS, BT, dt=BF16) for _ in range(2)]
        shift_f = [O_sb[0:H, b, :] for b in range(NB)]
        shift_bf = tmp(NB * BT // 2, NB, BT, dt=BF16)[0:H, :, :]
        shift_parts = shift_bf[:, 0:PARTS, :]
        vT = h_tm.rearrange("p (b a) d -> p b (a d)", b=NB)
        spare_sp = sp_tm.rearrange("p (b a) d -> p b (a d)", b=NB)
        qfs = [spare_sp[:, 0, :], spare_sp[:, 1, :]]
        rqs = [spare_sp[:, 2, :], spare_sp[:, 3, :]]
        sqqs = [v[:, BT // 2 * i:BT // 2 * (i + 1)].bitcast(BF16) for v in (num_T, den_T) for i in range(2)]
        second = Q_op[:, H * BT:2 * H * BT].bitcast(F32)
        hT = second[:, 0:NB * BT].rearrange("p (a b) -> p a b", a=NB)
        m1s = second[:, NB * BT:NB * BT + 2 * MH * BT].rearrange("p (a m b) -> p a m b", a=2, m=MH)
        k_parts = [probs[:, i, 0:PARTS * BT // 2].bitcast(BF16).rearrange("p (a b) -> p a b", a=PARTS)
                   for i in range(2)] + [tmp(PARTS * BT // 2, PARTS, BT, dt=BF16)]
        rks = [probs[:, 2, 0:BT], probs[:, 2, BT:2 * BT]]
        sqks = [probs[:, 3, BT // 2 * b:BT // 2 * (b + 1)].bitcast(BF16) for b in range(NB)]
        junk2 = probs[:, 3, BT:2 * BT]
        wg_i, wu_i = wg_f[:, :].bitcast(I32), wu_f[:, :].bitcast(I32)
        wd_i = wd_f[:, :, :].rearrange("p a b -> p (a b)").bitcast(I32)
        at[0] = over
        rec_T = tmp(BT)
        att_T = tmp(BT)
        junk = tmp(BT)
        x1 = tmp(BT, TPB, D)
        sp1 = tmp(BT, TPB, D)
        sq1 = tmp(BT, TPB, D)
        h2 = tmp(BT, TPB, D)
        h2_T = tmp(BT)
        th = [tmp(BT) for _ in range(NM)]
        gl = [tmp(BT) for _ in range(NM)]
        hid = tmp(NM * BT, NM, BT)
        y = tmp(BT, TPB, D)
        stat = sb("stat", [P, NT, 6])
        mv = sb("mv", [P, NT, 2])
        small = sb("small", [P, 16, NT])
        (rstd, n2, a2, y0, yc, t1, t2, rt, u, ln_u, nmr, dv0, inn, dn, fac, spare) = \
            (small[:, i, :] for i in range(16))
        kmax = sb("kmax", [P, 8])
        ok = sb("ok", [P, 3, NB])
        flag_f = sb("flag_f", [P, 4])
        flag_i = sb("flag_i", [P, 2], I32)
        mx = sb("mx", [P, TPB, H])

        ps = ctx.enter_context(nc.psum_tensor("ps", [P, 8, 512], F32))

        def bank(i):
            return ps[:, i, :]

        def slot_bank(s):
            return ps[:, 2 * s:2 * s + 2, :]

        O_bank, M_bank = bank(6), bank(7)

        names = """c_in wmod_in w_in hs_ready ffn_in const_ready pe_mod mod_ready silu_ready ffn_ready
        vec root_in root_out stat_ready xn_done ln_in ln_out h_ready v_ready
        hT_ps hT_sb m1_ps m1_sb m2_ps m2_sb vT_ps vT_sb k_ps q_ps v_ps
        k_hi k_res k_mid k_lo q_f q_hi q_res q_mid q_lo k_sq q_sq nk_ps nk_done nq_ps
        k_stored q_stored v_done kmax_ready bound shift_ready shift_stored K_filled Q_filled Q_loaded ones_ready
        scores exped pv_done o_evac norm wo_ps h2_done h2T_ps h2T_done gate_ps up_ps gate_th
        gated glu_done down_ps y_ready y_stored tail epow_in epow_out flag_in flag_ps flag_ready
        max_loaded shift_saved max_zero max_scores max_taken max_T""".split()
        S = {n: sem(n) for n in names}
        k_st = [[sem(f"k_st{i}{n}") for n in range(PARTS)] for i in range(3)]
        q_st = [sem(f"q_st{b}") for b in range(NB)]
        shift_st = [sem(f"shift_st{b}") for b in range(NB)]
        x_in = [sem(f"x_in{b}") for b in range(NB)]
        o_in = [sem(f"o_in{g}") for g in range(NG)]
        K_loaded = [sem(f"K_loaded{g}") for g in range(NG)]

        def q_slot(s):
            return lambda h: Q_op[:, bass.ds(s * (H * BT) + h * BT, BT)]

        block = ctx.enter_context(nc.Block())
        QUERY_LOADS = PARTS * PARTS + 1

        @block.sync
        def _(sp):
            xt = x.rearrange("(t p) d -> p t d", p=P)
            for b in range(NB):
                sp.dma_start(x_tm[:, TPB * b:TPB * (b + 1), :], xt[:, TPB * b:TPB * (b + 1), :]).then_inc(x_in[b], 16)

            for dst, src in ((fixed_sb[:, :], fixed), (w1_sb[:, :], w1t), (w2_sb[:, :, :], w2t),
                             (w_att_sb[:, :, :], w_att)):
                sp.dma_start(dst, src).then_inc(S["w_in"], 16)
            for dst, src in ((wg_i, wgt), (wu_i, wut), (wd_i, wdt)):
                sp.dma_start(dst, src).then_inc(S["ffn_in"], 16)

            def store_k(b):
                for n, part in enumerate(("k_hi", "k_mid", "k_lo")):
                    sp.wait_ge(S[part], b + 1)
                    sp.dma_start(k_scr[:, n, :, b * BT:(b + 1) * BT], k_parts[b % 3][:, n, :])\
                        .then_inc(k_st[b % 3][n], 16)

            def load_k(g):
                src = k_scr[GH * g:GH * (g + 1), :, :, :].rearrange("h a i t -> (a i) h t")
                for a in range(PARTS):
                    sp.dma_start(K_op[PARTS * DH * a:PARTS * DH * (a + 1), GH * g:GH * (g + 1), :], src)\
                        .then_inc(K_loaded[g], 16)

            def load_q(slot, b, loaded):
                q3 = Q_op[:, slot * H * BT:(slot + 1) * H * BT].rearrange("p (h t) -> p h t", h=H)
                tb = slice(b * BT, (b + 1) * BT)
                for s in range(PARTS * PARTS):
                    src = q_scr[s // PARTS, :, tb].rearrange("(h i) t -> i h t", i=DH)
                    sp.dma_start(q3[DH * s:DH * (s + 1), :, :], src).then_inc(loaded, 16)

            def load_shift(slot, b, loaded, parts):
                q3 = Q_op[:, slot * H * BT:(slot + 1) * H * BT].rearrange("p (h t) -> p h t", h=H)
                tb = slice(b * BT, (b + 1) * BT)
                sp.dma_start(q3[SHIFT_ROW:SHIFT_ROW + parts, :, :],
                             shift_scr[:, 0:parts, tb].rearrange("h a t -> a h t")).then_inc(loaded, 16)

            for b in range(NB):
                store_k(b)
            sp.wait_ge(S["K_filled"], 2)
            for i in range(3):
                for n in range(PARTS):
                    sp.wait_ge(k_st[i][n], 16 * len(range(i, NB, 3)))
            load_k(0)
            sp.wait_ge(S["q_lo"], 1)
            sp.dma_start(q_scr[:, :, 0:BT].rearrange("a f t -> f a t"), q_parts[0]).then_inc(q_st[0], 16)
            sp.wait_ge(q_st[0], 16)
            sp.wait_ge(S["Q_filled"], 1)
            load_q(0, 0, S["Q_loaded"])
            sp.wait_ge(S["shift_ready"], 1)
            sp.dma_start(shift_scr[:, 0, 0:BT], shift_bf[:, 0, :]).then_inc(shift_st[0], 16)
            sp.wait_ge(shift_st[0], 16)
            load_shift(0, 0, S["Q_loaded"], 1)
            for g in range(1, NG):
                sp.wait_ge(S["K_filled"], 2 * (g + 1))
                load_k(g)

            def gather(Bk, g):
                sp.wait_ge(S["o_evac"], NG * Bk + g + 1)
                if Bk % NB and g == 0:
                    sp.wait_ge(S["norm"], Bk)
                for j in range(GH):
                    rows = slice(GH * DH * g + DH * j, GH * DH * g + DH * (j + 1))
                    sp.dma_start(num_T[rows, :], O_sb[32 * j:32 * j + DH, g, :]).then_inc(o_in[g], 16)
                    sp.dma_start(den_T[rows, :], O_sb[32 * j + DH:32 * j + 2 * DH, g, :]).then_inc(o_in[g], 16)

            ot = out.rearrange("(t p) d -> p t d", p=P)

            def store(Bk):
                b = Bk % NB
                sp.wait_ge(S["y_ready"], Bk + 1)
                sp.dma_start(ot[:, TPB * b:TPB * (b + 1), :], y).then_inc(S["y_stored"], 16)

            def blocks(p):
                for b in range(NB):
                    Bk = NB * p + b
                    if b:
                        gather(Bk - 1, NG - 1)
                    if b + 1 < NB:
                        if not p:
                            sp.wait_ge(q_st[b + 1], 16)
                            sp.wait_ge(shift_st[b + 1], 16)
                            sp.wait_ge(S["Q_filled"], 2)
                        sp.wait_ge(S["Q_loaded"], 16 * QUERY_LOADS * (Bk + 1))
                        if Bk:
                            sp.wait_ge(S["scores"], 2 * STEPS * Bk)
                        load_q((b + 1) % 2, b + 1, S["Q_loaded"])
                        load_shift((b + 1) % 2, b + 1, S["Q_loaded"], PARTS if p else 1)
                    for g in range(NG - 1):
                        gather(Bk, g)
                        if b and g == 1:
                            store(Bk - 1)
                gather(NB * (p + 1) - 1, NG - 1)
                store(NB * (p + 1) - 1)
                sp.wait_ge(S["y_stored"], 16 * NB * (p + 1) + 1)

            blocks(0)

            sp.wait_ge(S["flag_ready"], 1)
            with sp.If(sp.value_load(flag_i[0:1, 0:1], min_val=0, max_val=1)):
                sp.wait_ge(S["max_zero"], 1)
                for b in range(NB):
                    sp.wait_ge(S["max_taken"], NT * GH * b + 1)
                    load_q(0, b, S["max_loaded"])
                    sp.wait_ge(S["max_loaded"], 16 * PARTS * PARTS * (b + 1))
                    sp.wait_ge(S["shift_ready"], NB + b + 1)
                    sp.dma_start(shift_scr[:, :, b * BT:(b + 1) * BT], shift_parts).then_inc(S["shift_saved"], 16)
                    sp.wait_ge(S["shift_saved"], 16 * (b + 1))
                load_q(0, 0, S["Q_loaded"])
                load_shift(0, 0, S["Q_loaded"], PARTS)
                blocks(1)

        @block.gpsimd
        def _(pool):
            pool.memset(half[:, :], 0.5).then_inc(S["const_ready"], 1)
            pool.memset(mhalf[:, :], -0.5).then_inc(S["const_ready"], 1)
            pool.memset(V_op[:, :, :], 1.0).then_inc(S["ones_ready"], 1)
            pool.wait_ge(S["const_ready"], 2)

            def root(dst, src, power, n, asked, done):
                pool.wait_ge(S[asked], n)
                pool.tensor_tensor(dst, src, power, ALU.pow).then_inc(S[done], 1)
                pool.wait_ge(S[done], n)

            def fill_k(g):
                hg = slice(GH * g, GH * (g + 1))
                pool.memset(K_op[64:96, hg, :].bitcast(F32), 0.0).then_inc(S["K_filled"], 1)
                pool.wait_ge(S["K_filled"], 2 * g + 1)
                pool.memset(K_op[96:128, hg, :].bitcast(F32), ONE_PAIR).then_inc(S["K_filled"], 1)
                pool.wait_ge(S["K_filled"], 2 * g + 2)

            pool.wait_ge(S["ones_ready"], 1)
            fill_k(0)
            pool.memset(Q_op[64:128, 0:H * BT].bitcast(F32), 0.0).then_inc(S["Q_filled"], 1)
            pool.wait_ge(S["Q_filled"], 1)
            pool.wait_ge(S["w_in"], 16 * 4)
            pool.tensor_copy(hs_bf[:, :], hs_sb).then_inc(S["hs_ready"], 1)
            pool.wait_ge(S["hs_ready"], 1)
            for g in range(1, NG):
                fill_k(g)
            for b in range(1, NB):
                pool.wait_ge(S["q_lo"], b + 1)
                pool.dma_start(q_scr[:, :, b * BT:(b + 1) * BT].rearrange("a f t -> f a t"), q_parts[b % 2])\
                    .then_inc(q_st[b], 16)
            pool.wait_ge(S["m2_ps"], NB)
            pool.memset(Q_op[64:128, H * BT:2 * H * BT].bitcast(F32), 0.0).then_inc(S["Q_filled"], 1)
            pool.wait_ge(S["Q_filled"], 2)
            for b in range(1, NB):
                pool.wait_ge(S["shift_ready"], b + 1)
                pool.dma_start(shift_scr[:, 0, b * BT:(b + 1) * BT], shift_bf[:, b, :]).then_inc(shift_st[b], 16)

            def tail_roots(Bk):
                r4 = slice(0, TPB)
                root(small[:, 1, r4], small[:, 2, r4], half[:, r4], 2 * Bk + 1, "epow_in", "epow_out")
                root(small[:, 3, r4], small[:, 4, r4], mhalf[:, r4], 2 * Bk + 2, "epow_in", "epow_out")

            with pool.Fori(0, NB) as b:
                tail_roots(b)

            pool.wait_ge(S["flag_ready"], 1)
            with pool.If(pool.value_load(flag_i[0:1, 0:1], min_val=0, max_val=1)):
                pool.memset(Q_op[96:128, 0:H * BT].bitcast(F32), 0.0).then_inc(S["max_zero"], 1)
                with pool.Fori(NB, 2 * NB) as b:
                    tail_roots(b)

        @block.scalar
        def _(act):
            act.dma_start(cols[:, 0:6], columns).then_inc(S["c_in"], 16)
            act.dma_start(wmod_sb[:, :], wmod).then_inc(S["wmod_in"], 16)
            act.wait_ge(S["c_in"], 16)
            act.activation(silu_c[:, 0:1], c_c, ACT.Exp, scale=-1.0).then_inc(S["silu_ready"], 1)

            def copy_hT(b):
                act.wait_ge(S["hT_ps"], b + 1)
                act.activation(hT[:, b, :], bank(b % 2), ACT.Identity, bias=mmu_c).then_inc(S["hT_sb"], 1)

            def tanh1(b):
                for m in range(MH):
                    act.wait_ge(S["m1_ps"], MH * b + m + 1)
                    if b >= 2:
                        act.wait_ge(S["m2_ps"], b - 1)
                    act.activation(m1s[:, b % 2, m, :], bank(M1_BANK[b][m]), ACT.Tanh, bias=b1_c[:, m:m + 1]).then_inc(S["m1_sb"], 1)

            def tanh2(b):
                act.wait_ge(S["m2_ps"], b + 1)
                act.activation(g_fm[:, b, :], bank(M2_BANK[b]), ACT.Tanh, bias=b2_c).then_inc(S["m2_sb"], 1)

            def root(dst, src, n):
                act.wait_ge(S["root_in"], n)
                act.activation(dst, src, ACT.Sqrt).then_inc(S["root_out"], 1)

            root(rt, spare, 1)
            act.wait_ge(S["stat_ready"], 1)
            for t in range(NT):
                act.activation(h_tm[:, t, :], x_tm[:, t, :], ACT.Identity, scale=rstd[:, t:t + 1],
                               bias=nmr[:, t:t + 1]).then_inc(S["xn_done"], 1)
            for b in range(NB):
                copy_hT(b)
            root(y0, a2, 2)
            root(rt, t2, 3)
            root(dn, inn, 4)
            act.wait_ge(S["ln_in"], 1)
            act.activation(ln_u, u, ACT.Ln).then_inc(S["ln_out"], 1)

            def copy_vT(b):
                act.wait_ge(S["vT_ps"], b + 1)
                act.activation(vT[:, b, :], bank(b % 2), ACT.Identity).then_inc(S["vT_sb"], 1)

            def k_split1(b):
                act.wait_ge(S["k_ps"], b + 1)
                if b == 3:
                    for n in range(PARTS):
                        act.wait_ge(k_st[0][n], 16)
                act.activation(k_parts[b % 3][:, 0, :], bank(2 + b % 2), ACT.Identity).then_inc(S["k_hi"], 1)
                act.activation(sqks[b], bank(2 + b % 2), ACT.Square).then_inc(S["k_sq"], 1)

            def k_split2(b):
                act.wait_ge(S["k_res"], b + 1)
                act.activation(k_parts[b % 3][:, 1, :], rks[b % 2], ACT.Identity).then_inc(S["k_mid"], 1)

            def q_split1(b):
                act.wait_ge(S["q_f"], b + 1)
                if b >= 2:
                    act.wait_ge(q_st[b - 2], 16)
                act.activation(q_parts[b % 2][:, 0, :], qfs[b % 2], ACT.Identity).then_inc(S["q_hi"], 1)
                act.activation(sqqs[b], qfs[b % 2], ACT.Square).then_inc(S["q_sq"], 1)

            def q_split2(b):
                act.wait_ge(S["q_res"], b + 1)
                act.activation(q_parts[b % 2][:, 1, :], rqs[b % 2], ACT.Identity).then_inc(S["q_mid"], 1)

            def bound(b):
                act.wait_ge(S["nq_ps"], b + 1)
                act.wait_ge(S["kmax_ready"], 1)
                act.activation(shift_f[b], bank(NQ_BANK[b])[0:H, :], ACT.Sqrt, scale=kmax[0:H, NB:NB + 1])\
                    .then_inc(S["bound"], 1)

            tanh1(0)
            tanh1(1)
            tanh2(0)
            copy_vT(0)
            tanh2(1)
            copy_vT(1)
            k_split1(0)
            copy_vT(2)
            k_split2(0)
            k_split1(1)
            tanh1(2)
            k_split2(1)
            copy_vT(3)
            k_split1(2)
            tanh2(2)
            k_split2(2)
            k_split1(3)
            tanh1(3)
            k_split2(3)
            q_split1(0)
            q_split2(0)
            tanh2(3)
            bound(0)
            for b in range(1, NB):
                q_split1(b)
                q_split2(b)
            for b in range(1, NB):
                bound(b)
            act.wait_ge(S["q_lo"], NB)

            def block_steps(Bk, tails):
                for j in range(STEPS):
                    for half_ in range(2):
                        u = 2 * j + half_
                        act.wait_ge(S["scores"], Bk * 2 * STEPS + u + 1)
                        act.activation(probs[:, 2 * (j % 2) + half_, :], slot_bank(u % 3), ACT.Exp)\
                            .then_inc(S["exped"], 1)
                    if tails:
                        if j == AT_TR:
                            copy_h2(Bk - 1)
                        if j in AT_GATE:
                            gate(Bk - 1, AT_GATE.index(j), M_bank)

            def copy_h2(Bk):
                act.wait_ge(S["h2T_ps"], Bk + 1)
                act.activation(h2_T, M_bank, ACT.Identity).then_inc(S["h2T_done"], 1)

            def gate(Bk, m, from_bank):
                act.wait_ge(S["gate_ps"], Bk * NM + m + 1)
                act.activation(th[m], from_bank, ACT.Tanh, scale=0.5).then_inc(S["gate_th"], 1)

            def blocks(p):
                block_steps(NB * p, False)
                with act.Fori(NB * p + 1, NB * (p + 1)) as Bk:
                    block_steps(Bk, True)
                last = NB * (p + 1) - 1
                copy_h2(last)
                for m in range(NM):
                    gate(last, m, bank(m))

            blocks(0)
            act.wait_ge(S["flag_ready"], 1)
            with act.If(act.value_load(flag_i[0:1, 0:1], min_val=0, max_val=1)):
                blocks(1)

        @block.tensor
        def _(pe):
            pe.wait_ge(S["mod_ready"], 1)
            pe.wait_ge(S["wmod_in"], 16)
            for i in range(2):
                ins = pe.matmul(bank(6 + i)[:, 0:3 * D], silu_b[:, :], wmod_sb[:, 3 * D * i:3 * D * (i + 1)],
                                start=True, stop=True)
            ins.then_inc(S["pe_mod"], 1)
            pe.wait_ge(S["w_in"], 16 * 4)

            def transposes(src, b, done):
                for t in range(TPB):
                    ins = pe.transpose(bank(b % 2)[:, P * t:P * (t + 1)], src[:, TPB * b + t, :], ident_sb)
                ins.then_inc(S[done], 1)

            def metric_T(b):
                pe.wait_ge(S["h_ready"], b + 1)
                if b >= 2:
                    pe.wait_ge(S["hT_sb"], b - 1)
                transposes(h_tm, b, "hT_ps")

            def metric(b):
                pe.wait_ge(S["hT_sb"], b + 1)
                for m in range(MH):
                    if b == 2:
                        pe.wait_ge(S["m2_sb"], m + 1)
                    if b == 3:
                        pe.wait_ge(*((S["m1_sb"], MH * b) if m == 0 else (S["m2_sb"], b)))
                    pe.matmul(bank(M1_BANK[b][m]), w1_sb[:, P * m:P * (m + 1)], hT[:, b, :], start=True, stop=True)\
                        .then_inc(S["m1_ps"], 1)

            def metric2(b):
                pe.wait_ge(S["m1_sb"], MH * (b + 1))
                for m in range(MH):
                    ins = pe.matmul(bank(M2_BANK[b]), w2_sb[:, m, :], m1s[:, b % 2, m, :],
                                    start=m == 0, stop=m == MH - 1)
                ins.then_inc(S["m2_ps"], 1)

            for b in range(NB):
                metric_T(b)
            metric(0)
            metric(1)

            def v_T(b):
                pe.wait_ge(S["v_ready"], b + 1)
                pe.wait_ge(S["hT_sb"], NB)
                if b >= 2:
                    pe.wait_ge(S["vT_sb"], b - 1)
                transposes(sp_tm, b, "vT_ps")

            def k_of(b):
                pe.wait_ge(S["vT_sb"], b + 1)
                if b >= 2:
                    pe.wait_ge(S["k_res"], b - 1)
                pe.matmul(bank(2 + b % 2), wk_sb, vT[:, b, :], start=True, stop=True).then_inc(S["k_ps"], 1)

            def v_of(b):
                if b >= 2:
                    pe.wait_ge(S["v_done"], b - 1)
                for t in range(TPB):
                    ins = pe.matmul(bank(4 + b % 2)[:, P * t:P * (t + 1)], vT[:, b, P * t:P * (t + 1)], wv_sb,
                                    start=True, stop=True)
                ins.then_inc(S["v_ps"], 1)

            def nk(b):
                pe.wait_ge(S["k_sq"], b + 1)
                if b:
                    pe.wait_ge(S["nk_done"], b)
                pe.matmul(bank(0)[0:H, :], hs_bf[:, :], sqks[b], start=True, stop=True).then_inc(S["nk_ps"], 1)

            def q_of(b):
                if b:
                    pe.wait_ge(S["q_f"], b)
                pe.matmul(bank(1), wq_sb, vT[:, b, :], start=True, stop=True).then_inc(S["q_ps"], 1)

            def nq(b):
                pe.wait_ge(S["q_sq"], b + 1)
                pe.matmul(bank(NQ_BANK[b])[0:H, :], hs_bf[:, :], sqqs[b], start=True, stop=True).then_inc(S["nq_ps"], 1)

            metric2(0)
            v_T(0)
            metric2(1)
            v_T(1)
            k_of(0)
            v_of(0)
            k_of(1)
            v_of(1)
            v_T(2)
            metric(2)
            v_T(3)
            k_of(2)
            v_of(2)
            metric2(2)
            k_of(3)
            v_of(3)
            pe.wait_ge(S["vT_sb"], NB)
            pe.wait_ge(S["hs_ready"], 1)
            nk(0)
            q_of(0)
            metric(3)
            for b in range(1, NB):
                nk(b)
            pe.wait_ge(S["k_res"], NB)
            pe.wait_ge(S["v_done"], NB)
            nq(0)
            metric2(3)
            for b in range(1, NB):
                q_of(b)
                nq(b)

            def score(Bk, j):
                start = isinstance(Bk, int) and Bk == 0
                g, kt = divmod(j, NT)
                if kt == 0 and start:
                    pe.wait_ge(K_loaded[g], 16 * PARTS)
                queries = q_slot(Bk % 2)
                for half_ in range(2):
                    u = 2 * j + half_
                    if u >= 3:
                        pe.wait_ge(S["exped"], Bk * 2 * STEPS + u - 2)
                    elif u < 2 and not start:
                        pe.wait_ge(S["exped"], Bk * 2 * STEPS + u - 1)
                    for i in range(2):
                        h = GH * g + 2 * half_ + i
                        ins = pe.matmul(slot_bank(u % 3)[:, i, :], K_op[:, h, P * kt:P * (kt + 1)], queries(h),
                                        start=True, stop=True)
                    ins.then_inc(S["scores"], 1)

            def product(Bk, j):
                g, kt = divmod(j, NT)
                pe.wait_ge(S["exped"], Bk * 2 * STEPS + 2 * j + 2)
                if kt == 0 and not (isinstance(Bk, int) and Bk == 0 and g == 0):
                    pe.wait_ge(S["o_evac"], Bk * NG + g)
                for i in range(GH):
                    h = GH * g + i
                    ins = pe.matmul(O_bank[32 * i:32 * (i + 1), :], V_op[:, kt, VW * h:VW * h + 32],
                                    probs[:, 2 * (j % 2) + i // 2, BT * (i % 2):BT * (i % 2 + 1)],
                                    start=kt == 0, stop=kt == NT - 1, tile_position=(0, 32 * i))
                if kt == NT - 1:
                    ins.then_inc(S["pv_done"], 1)

            def t_wo(Bk):
                pe.wait_ge(S["norm"], Bk + 1)
                for t in range(TPB):
                    ins = pe.matmul(M_bank[:, P * t:P * (t + 1)], att_T[:, P * t:P * (t + 1)], wo_sb,
                                    start=True, stop=True)
                ins.then_inc(S["wo_ps"], 1)

            def t_transpose(Bk):
                pe.wait_ge(S["h2_done"], Bk + 1)
                for t in range(TPB):
                    ins = pe.transpose(M_bank[:, P * t:P * (t + 1)], h2[:, t, :], ident_sb)
                ins.then_inc(S["h2T_ps"], 1)

            def t_gate(Bk, m, to):
                pe.wait_ge(S["h2T_done"], Bk + 1)
                if m and to is M_bank:
                    pe.wait_ge(S["glu_done"], Bk * NM + m)
                pe.matmul(to, wg_f[:, P * m:P * (m + 1)], h2_T, start=True, stop=True).then_inc(S["gate_ps"], 1)

            def t_up(Bk, m, to):
                if to is M_bank:
                    pe.wait_ge(S["gated"], Bk * NM + m + 1)
                pe.matmul(to, wu_f[:, P * m:P * (m + 1)], h2_T, start=True, stop=True).then_inc(S["up_ps"], 1)

            def t_down(Bk, to):
                pe.wait_ge(S["glu_done"], Bk * NM + NM)
                for t in range(TPB):
                    for m in range(NM):
                        ins = pe.matmul(to[:, P * t:P * (t + 1)], hid[:, m, P * t:P * (t + 1)], wd_f[:, m, :],
                                        start=m == 0, stop=m == NM - 1)
                ins.then_inc(S["down_ps"], 1)

            def block_steps(Bk, tails):
                for j in range(STEPS):
                    score(Bk, j)
                    if j:
                        product(Bk, j - 1)
                    elif tails:
                        product(Bk - 1, STEPS - 1)
                    if tails:
                        if j == AT_WO:
                            t_wo(Bk - 1)
                        if j == AT_TR:
                            t_transpose(Bk - 1)
                        if j in AT_GATE:
                            t_gate(Bk - 1, AT_GATE.index(j), M_bank)
                        if j in AT_UP:
                            t_up(Bk - 1, AT_UP.index(j), M_bank)
                        if j == AT_DOWN:
                            t_down(Bk - 1, M_bank)

            def blocks(p):
                first, last = NB * p, NB * (p + 1) - 1
                pe.wait_ge(S["Q_loaded"], 16 * QUERY_LOADS * (first + 1))
                block_steps(first, False)
                if p == 0:
                    pe.wait_ge(S["ffn_ready"], 3)
                with pe.Fori(first + 1, last + 1) as Bk:
                    pe.wait_ge(S["Q_loaded"], 16 * QUERY_LOADS * (Bk + 1))
                    block_steps(Bk, True)
                product(last, STEPS - 1)
                t_wo(last)
                t_transpose(last)
                for m in range(NM):
                    t_gate(last, m, bank(m))
                    t_up(last, m, bank(3 + m))
                if p == 0:
                    pe.wait_ge(S["flag_in"], 1)
                    pe.matmul(M_bank[0:1, 0:1], flag_f[:, 0:1], flag_f[:, 1:2], start=True, stop=True)\
                        .then_inc(S["flag_ps"], 1)
                t_down(last, bank(6))

            for done in ("vT_sb", "k_res", "v_done", "nk_done", "q_f", "bound"):
                pe.wait_ge(S[done], NB)
            blocks(0)

            pe.wait_ge(S["flag_ready"], 1)
            with pe.If(pe.value_load(flag_i[0:1, 0:1], min_val=0, max_val=1)):
                q_all = q_slot(0)
                with pe.Fori(0, NB) as b:
                    pe.wait_ge(S["max_loaded"], 16 * PARTS * PARTS * (b + 1))
                    for h in range(H):
                        for t in range(TPB):
                            pe.wait_ge(S["max_taken"], b * (H * TPB) + h * TPB + t + 1)
                            for i in range(NB):
                                ins = pe.matmul(bank(i), q_all(h)[:, P * t:P * (t + 1)],
                                                K_op[:, h, BT * i:BT * (i + 1)], start=True, stop=True)
                            ins.then_inc(S["max_scores"], 1)
                    pe.wait_ge(S["max_taken"], (b + 1) * (H * TPB) + 1)
                    for t in range(TPB):
                        ins = pe.transpose(M_bank[0:H, P * t:P * (t + 1)], mx[:, t, :], ident_sb)
                    ins.then_inc(S["max_T"], 1)
                blocks(1)

        @block.vector
        def _(dve):
            vec = Chain(dve, S["vec"])

            def row3(m, n):
                return mod[:, D * m:D * (m + 1)].unsqueeze(1).to_broadcast([P, n, D])

            def split_shift(c, sf, parts):
                c.after()
                c.did(dve.tensor_copy(parts[:, 0, :], sf))
                c.after()
                c.did(dve.tensor_tensor(sf, sf, parts[:, 0, :], ALU.subtract))
                c.after()
                c.did(dve.tensor_copy(parts[:, 1, :], sf))
                c.after()
                dve.tensor_tensor(parts[:, 2, :], sf, parts[:, 1, :], ALU.subtract).then_inc(S["shift_ready"], 1)

            def newton(dst, rough, a, tmp_):
                vec.did(dve.reciprocal(tmp_, rough))
                vec.after()
                vec.did(dve.scalar_tensor_tensor(tmp_, a, 0.5, tmp_, ALU.mult, ALU.mult))
                vec.after()
                vec.did(dve.scalar_tensor_tensor(dst, rough, 0.5, tmp_, ALU.mult, ALU.add))
                vec.after()

            vec.did(dve.memset(ones_bf[:, :], 1.0))
            vec.did(dve.memset(ok[:, :, :], 1.0))
            vec.did(dve.memset(flag_f[:, :], 1.0))
            for b in range(NB):
                dve.wait_ge(x_in[b], 16)
                for t in range(TPB * b, TPB * (b + 1)):
                    vec.did(dve.bn_stats(stat[:, t, :], x_tm[:, t, :]))
                if b == 1:
                    dve.wait_ge(S["silu_ready"], 1)
                    vec.did(dve.tensor_scalar(silu_c[:, 1:2], silu_c[:, 0:1], 1.0, None, ALU.add))
                    vec.after()
                    vec.did(dve.reciprocal(silu_c[:, 0:1], silu_c[:, 1:2]))
                    vec.after()
                    dve.tensor_scalar(silu_b[:, :], ones_bf[:, 0:P], silu_c[:, 0:1], c_c, ALU.mult, ALU.mult)\
                        .then_inc(S["mod_ready"], 1)
            vec.after()
            for t in range(NT):
                vec.did(dve.bn_aggr(mv[:, t, :], stat[:, t, :]))
            vec.after()
            dve.tensor_scalar(spare, mv[:, :, 1], LN_EPS, None, ALU.add).then_inc(S["root_in"], 1)
            dve.wait_ge(S["pe_mod"], 1)
            vec.did(dve.tensor_copy(mod[:, 0:3 * D], bank(6)[:, 0:3 * D]))
            vec.did(dve.tensor_copy(mod[:, 3 * D:6 * D], bank(7)[:, 0:3 * D]))
            vec.after()
            for m in (1, 4):
                vec.did(dve.tensor_scalar(mod[:, D * m:D * (m + 1)], mod[:, D * m:D * (m + 1)], 1.0, None, ALU.add))
            dve.wait_ge(S["root_out"], 1)
            newton(a2, rt, spare, t1)
            vec.did(dve.reciprocal(rstd, a2))
            vec.after()
            dve.scalar_tensor_tensor(nmr, mv[:, :, 0], -1.0, rstd, ALU.mult, ALU.mult).then_inc(S["stat_ready"], 1)
            for m in (2, 5):
                gate = mod[:, D * m:D * (m + 1)]
                sign, size = junk2[:, 0:P], junk2[:, P:2 * P]
                vec.did(dve.tensor_scalar(sign, gate, 0.0, 2.0, ALU.is_ge, ALU.mult))
                vec.did(dve.scalar_tensor_tensor(size, gate, -1.0, gate, ALU.mult, ALU.max))
                vec.after()
                vec.did(dve.tensor_scalar(sign, sign, -1.0, None, ALU.add))
                vec.after()
                vec.did(dve.scalar_tensor_tensor(gate, size, 0.25, sign, ALU.max, ALU.mult))
                vec.after()
            for b in range(NB):
                hb, spb = h_tm[:, TPB * b:TPB * (b + 1), :], sp_tm[:, TPB * b:TPB * (b + 1), :]
                dve.wait_ge(S["xn_done"], TPB * (b + 1))
                vec.did(dve.tensor_tensor(hb, hb, row3(1, TPB), ALU.mult))
                vec.after()
                dve.tensor_tensor(hb, hb, row3(0, TPB), ALU.add).then_inc(S["h_ready"], 1)
                dve.wait_ge(S["h_ready"], b + 1)
                vec.did(dve.tensor_scalar(spb, hb, 8.0, -8.0, ALU.min, ALU.max))
                vec.after()
                for t in range(TPB * b, TPB * (b + 1)):
                    vec.did(dve.tensor_tensor_reduce(junk2[:, P * (t % TPB) + 1:P * (t % TPB + 1)],
                                                     sp_tm[:, t, 1:D], sp_tm[:, t, 1:D], 1.0, 0.0,
                                                     ALU.mult, ALU.add, n2[:, t:t + 1]))
            vec.after()
            dve.tensor_scalar(a2, n2, 1.0, EPS, ALU.add, ALU.add).then_inc(S["root_in"], 1)
            dve.wait_ge(S["root_out"], 2)
            newton(y0, y0, a2, t1)
            vec.did(dve.tensor_scalar(yc, y0, 1.0 + EPS, None, ALU.max))
            vec.after()
            vec.did(dve.tensor_scalar(t1, yc, -1.0, None, ALU.add))
            vec.after()
            dve.scalar_tensor_tensor(t2, yc, 1.0, t1, ALU.add, ALU.mult).then_inc(S["root_in"], 1)
            vec.did(dve.tensor_tensor(dv0, y0, yc, ALU.subtract))
            vec.after()
            dve.wait_ge(S["root_in"], 3)
            vec.did(dve.tensor_tensor(t1, dv0, dv0, ALU.mult))
            vec.after()
            vec.did(dve.tensor_tensor(t1, n2, t1, ALU.subtract))
            vec.after()
            dve.tensor_scalar(inn, t1, EPS, None, ALU.max).then_inc(S["root_in"], 1)
            dve.wait_ge(S["root_in"], 4)
            dve.wait_ge(S["root_out"], 3)
            newton(rt, rt, t2, t1)
            dve.tensor_tensor(u, yc, rt, ALU.add).then_inc(S["ln_in"], 1)
            dve.wait_ge(S["root_out"], 4)
            newton(dn, dn, inn, t1)
            vec.did(dve.tensor_scalar(t1, dn, EPS, None, ALU.add))
            vec.after()
            vec.did(dve.reciprocal(fac, t1))
            vec.after()
            dve.wait_ge(S["ln_out"], 1)
            vec.did(dve.scalar_tensor_tensor(fac, ln_u, 0.001, fac, ALU.max, ALU.mult))
            vec.after()
            vec.did(dve.tensor_tensor(sp_tm[:, :, 0], dv0, fac, ALU.mult))
            for b in range(NB):
                for t in range(TPB * b, TPB * (b + 1)):
                    ins = dve.tensor_scalar(sp_tm[:, t, 1:D], sp_tm[:, t, 1:D], fac[:, t:t + 1], None, ALU.mult)
                    if t % TPB < TPB - 1:
                        vec.did(ins)
                ins.then_inc(S["v_ready"], 1)

            def metric(b):
                dve.wait_ge(S["m2_sb"], b + 1)
                vec.did(dve.tensor_scalar(g_fm[:, b, :], g_fm[:, b, :], 0.1, eta_c, ALU.mult, ALU.add))
                vec.after()
                vec.did(dve.scalar_tensor_tensor(g_fm[:, b, :], g_fm[:, b, :], -1.0, g_fm[:, b, :],
                                                 ALU.mult, ALU.max))
                vec.after()

            def queries(b):
                dve.wait_ge(S["q_ps"], b + 1)
                if b >= 2:
                    dve.wait_ge(S["q_sq"], b - 1)
                    dve.wait_ge(S["q_res"], b - 1)
                dve.scalar_tensor_tensor(qfs[b % 2], bank(1), eta_s, g_fm[:, b, :], ALU.mult, ALU.mult)\
                    .then_inc(S["q_f"], 1)

            def queries_rest(b):
                dve.wait_ge(S["q_hi"], b + 1)
                if b >= 2:
                    dve.wait_ge(S["q_mid"], b - 1)
                    dve.wait_ge(S["q_lo"], b - 1)
                dve.wait_ge(S["q_f"], b + 1)
                dve.tensor_tensor(rqs[b % 2], qfs[b % 2], q_parts[b % 2][:, 0, :], ALU.subtract)\
                    .then_inc(S["q_res"], 1)

            def queries_low(b):
                dve.wait_ge(S["q_mid"], b + 1)
                dve.wait_ge(S["q_res"], b + 1)
                dve.tensor_tensor(q_parts[b % 2][:, 2, :], rqs[b % 2], q_parts[b % 2][:, 1, :], ALU.subtract)\
                    .then_inc(S["q_lo"], 1)

            def k_max(b):
                dve.wait_ge(S["nk_ps"], b + 1)
                dve.tensor_reduce(kmax[0:H, b:b + 1], bank(0)[0:H, :], AX.X, ALU.max).then_inc(S["nk_done"], 1)

            def shift(b):
                dve.wait_ge(S["bound"], b + 1)
                dve.tensor_scalar(shift_bf[:, b, :], shift_f[b], -1.0 - 2.0 ** -7, HEADROOM, ALU.mult, ALU.add)\
                    .then_inc(S["shift_ready"], 1)

            vec.did(dve.tensor_scalar(eta_s, eta_c, DH ** -0.5, None, ALU.mult))
            def k_rest(b):
                dve.wait_ge(S["k_sq"], b + 1)
                if b >= 2:
                    dve.wait_ge(S["k_mid"], b - 1)
                    dve.wait_ge(S["k_lo"], b - 1)
                dve.tensor_tensor(rks[b % 2], bank(2 + b % 2), k_parts[b % 3][:, 0, :], ALU.subtract)\
                    .then_inc(S["k_res"], 1)

            def k_low(b):
                dve.wait_ge(S["k_mid"], b + 1)
                dve.wait_ge(S["k_res"], b + 1)
                dve.tensor_tensor(k_parts[b % 3][:, 2, :], rks[b % 2], k_parts[b % 3][:, 1, :], ALU.subtract)\
                    .then_inc(S["k_lo"], 1)

            def values(b):
                dve.wait_ge(S["v_ps"], b + 1)
                for t in range(TPB):
                    ins = dve.tensor_copy(
                        V_op[:, TPB * b + t, 0:H * VW].rearrange("p (h w) -> p h w", h=H)[:, :, 0:DH],
                        bank(4 + b % 2)[:, P * t:P * (t + 1)].rearrange("p (h i) -> p h i", h=H))
                    if t < TPB - 1:
                        vec.did(ins)
                ins.then_inc(S["v_done"], 1)

            dve.wait_ge(S["ones_ready"], 1)
            for b in range(NB):
                k_rest(b)
                values(b)
                k_low(b)
                if b < 3:
                    metric(b)
            k_max(0)
            queries(0)
            k_max(1)
            queries_rest(0)
            k_max(2)
            k_max(3)
            queries_low(0)
            dve.wait_ge(S["nk_done"], NB)
            dve.tensor_reduce(kmax[0:H, NB:NB + 1], kmax[0:H, 0:NB], AX.X, ALU.max).then_inc(S["kmax_ready"], 1)
            queries(1)
            queries_rest(1)
            shift(0)
            metric(3)
            queries_low(1)
            for b in range(2, NB):
                queries(b)
                queries_rest(b)
                queries_low(b)
            for b in range(1, NB):
                shift(b)
            dve.wait_ge(S["ffn_in"], 16 * 3)
            dve.tensor_scalar(wg_f[:, :], wg_i, FFN_SCALE, None, ALU.mult).then_inc(S["ffn_ready"], 1)
            dve.tensor_scalar(wu_f[:, :], wu_i, FFN_SCALE, None, ALU.mult).then_inc(S["ffn_ready"], 1)
            dve.tensor_scalar(wd_f[:, :, :].rearrange("p a b -> p (a b)"), wd_i, FFN_SCALE, 0.5, ALU.mult, ALU.mult)\
                .then_inc(S["ffn_ready"], 1)

            def evacuate(Bk, g):
                dve.wait_ge(S["pv_done"], Bk * NG + g + 1)
                dve.tensor_copy(O_sb[:, g, :], O_bank).then_inc(S["o_evac"], 1)

            TAIL_STEPS = 29

            class Tail:
                def __init__(self, Bk, b):
                    self.Bk, self.b = Bk, b
                    self.c = Chain(dve, S["tail"], Bk * TAIL_STEPS)

                def normalise(self):
                    Bk, c = self.Bk, self.c
                    for g in range(NG):
                        dve.wait_ge(o_in[g], 16 * 2 * GH * (Bk + 1))
                    c.did(dve.reciprocal(rec_T, den_T))
                    c.did(dve.tensor_scalar(junk, den_T, SUM_FLOOR, None, ALU.is_ge, ALU.min, accum_out=ok[:, 1, 0:1]))
                    c.after()
                    dve.tensor_tensor(att_T, num_T, rec_T, ALU.mult).then_inc(S["norm"], 1)
                    c.did(dve.tensor_scalar(junk, num_T, BIG, None, ALU.is_le, ALU.min, accum_out=ok[:, 1, 1:2]))
                    c.after()
                    c.did(dve.tensor_scalar(junk, num_T, -BIG, None, ALU.is_ge, ALU.min, accum_out=ok[:, 1, 2:3]))
                    c.after()
                    c.did(dve.tensor_tensor(ok[:, 0, 0:3], ok[:, 0, 0:3], ok[:, 1, 0:3], ALU.min))

                def residual(self):
                    Bk, c = self.Bk, self.c
                    r4 = slice(0, TPB)
                    x0, arg, rs, var = (small[:, i, r4] for i in (1, 2, 3, 4))
                    flat = sp1.rearrange("p a b -> p (a b)")
                    dve.wait_ge(S["wo_ps"], Bk + 1)
                    c.did(dve.tensor_scalar(flat, M_bank, 0.1, 8.0, ALU.mult, ALU.min))
                    c.after()
                    c.did(dve.tensor_scalar(flat, flat, -8.0, None, ALU.max))
                    c.after()
                    for t in range(TPB):
                        c.did(dve.tensor_tensor_reduce(sq1[:, t, 1:D], sp1[:, t, 1:D], sp1[:, t, 1:D], 1.0, 0.0,
                                                       ALU.mult, ALU.add, var[:, t:t + 1]))
                    c.after()
                    dve.tensor_scalar(arg, var, 1.0, EPS, ALU.add, ALU.add).then_inc(S["epow_in"], 1)
                    dve.wait_ge(S["epow_out"], 2 * Bk + 1)
                    c.did(dve.tensor_copy(sp1[:, :, 0], x0))
                    c.after()
                    c.did(dve.tensor_tensor(x1, sp1, row3(2, TPB), ALU.mult))
                    c.after()
                    c.did(dve.tensor_tensor(x1, x1, x_tm[:, bass.ds(TPB * self.b, TPB), :], ALU.add))
                    c.after()
                    for t in range(TPB):
                        c.did(dve.bn_stats(stat[:, t, :], x1[:, t, :]))
                    c.after()
                    c.did(dve.tensor_copy(junk[:, 0:1], stat[:, 0, 0:1]))
                    for t in range(TPB):
                        c.did(dve.bn_aggr(mv[:, t, :], stat[:, t, :]))
                    c.after()
                    dve.tensor_scalar(var, mv[:, r4, 1], LN_EPS, None, ALU.add).then_inc(S["epow_in"], 1)
                    dve.wait_ge(S["epow_out"], 2 * Bk + 2)
                    for t in range(TPB):
                        c.did(dve.tensor_scalar(h2[:, t, :], x1[:, t, :], mv[:, t, 0:1], rs[:, t:t + 1],
                                                ALU.subtract, ALU.mult))
                    c.after()
                    c.did(dve.tensor_tensor(h2, h2, row3(4, TPB), ALU.mult))
                    c.after()
                    dve.tensor_tensor(h2, h2, row3(3, TPB), ALU.add).then_inc(S["h2_done"], 1)

                def gated(self, m, gates):
                    n = self.Bk * NM + m
                    dve.wait_ge(S["gate_th"], n + 1)
                    dve.scalar_tensor_tensor(gl[m], th[m], 1.0, gates, ALU.add, ALU.mult).then_inc(S["gated"], 1)

                def glu(self, m, ups):
                    n = self.Bk * NM + m
                    dve.wait_ge(S["gated"], n + 1)
                    dve.wait_ge(S["up_ps"], n + 1)
                    dve.tensor_tensor(hid[:, m, :], ups, gl[m], ALU.mult).then_inc(S["glu_done"], 1)

                def result(self, downs):
                    Bk, c = self.Bk, self.c
                    dve.wait_ge(S["down_ps"], Bk + 1)
                    dve.wait_ge(S["y_stored"], 16 * Bk + 1)
                    c.did(dve.tensor_tensor(y, downs.rearrange("p (a b) -> p a b", a=TPB), row3(5, TPB), ALU.mult))
                    c.after()
                    dve.tensor_tensor(y, y, x1, ALU.add).then_inc(S["y_ready"], 1)
                    assert c.n == TAIL_STEPS, c.n

            def blocks(p):
                for g in range(NG - 1):
                    evacuate(NB * p, g)
                if p == 0:
                    for b in range(NB):
                        dve.wait_ge(q_st[b], 16)
                        dve.wait_ge(shift_st[b], 16)
                with dve.Fori(NB * p + 1, NB * (p + 1)) as Bk:
                    evacuate(Bk - 1, NG - 1)
                    tail = Tail(Bk - 1, Bk - 1 - NB * p)
                    tail.normalise()
                    tail.residual()
                    evacuate(Bk, 0)
                    for m in range(NM):
                        tail.gated(m, M_bank)
                        tail.glu(m, M_bank)
                    evacuate(Bk, 1)
                    tail.result(M_bank)
                    evacuate(Bk, 2)
                last = NB * (p + 1) - 1
                evacuate(last, NG - 1)
                tail = Tail(last, NB - 1)
                tail.normalise()
                if p == 0:
                    tail.c.after()
                    dve.tensor_reduce(flag_f[:, 0:1], ok[:, 0, 0:3], AX.X, ALU.min).then_inc(S["flag_in"], 1)
                tail.residual()
                for m in range(NM):
                    tail.gated(m, bank(m))
                    tail.glu(m, bank(3 + m))
                if p == 0:
                    dve.wait_ge(S["flag_ps"], 1)
                    dve.tensor_scalar(flag_i[0:1, 0:1], M_bank[0:1, 0:1], P - 0.5, None, ALU.is_lt)\
                        .then_inc(S["flag_ready"], 1)
                tail.result(bank(6))

            dve.memset(mx[:, :, :], 0.0).then_inc(S["max_taken"], 1)
            vec.after()
            dve.tensor_copy(flag_f[:, 2:3], flag_f[:, 1:2]).then_inc(S["y_stored"], 1)
            blocks(0)

            dve.wait_ge(S["flag_ready"], 1)
            with dve.If(dve.value_load(flag_i[0:1, 0:1], min_val=0, max_val=1)):
                MAX_STEPS = 4
                with dve.Fori(0, NB) as b:
                    for h in range(H):
                        for t in range(TPB):
                            dve.wait_ge(S["max_scores"], b * (H * TPB) + h * TPB + t + 1)
                            dve.tensor_reduce(mx[:, t, h:h + 1], ps[:, 0:NB, :], AX.XY, ALU.max)\
                                .then_inc(S["max_taken"], 1)
                    c = Chain(dve, S["vec"], b * MAX_STEPS + vec.n)
                    dve.wait_ge(S["max_T"], b + 1)
                    c.did(dve.tensor_scalar(shift_f[0], M_bank[0:H, :], -1.0, None, ALU.mult))
                    split_shift(c, shift_f[0], shift_parts)
                    assert c.n == MAX_STEPS
                    dve.wait_ge(S["shift_saved"], 16 * (b + 1))
                blocks(1)


_NAMES = ["x", "columns", "wmod", "fixed", "w1t", "w2t", "w_att", "wgt", "wut", "wdt"]


def kernel(**inputs):
    import concourse.bacc as _bacc
    from concourse.bass_utils import run_bass_kernel_spmd as _run

    a = {k: np.asarray(v) for k, v in inputs.items()}
    eta = np.ones((D, 1), np.float32)
    eta[0] = -1.0
    mu = np.zeros((D, 1), np.float32)
    mu[0] = 1.0
    heads = np.repeat(np.eye(H, dtype=np.float32), DH, axis=0)
    lay = {
        "x": a["L0_attn_x"][0],
        "columns": np.concatenate([a["L0_attn_b1"].reshape(MH, P).T, a["L0_attn_b2"].reshape(D, 1), eta, -mu,
                                   a["L0_c"].reshape(D, 1)], axis=1),
        "wmod": a["L0_wmod"],
        "fixed": np.concatenate([np.eye(P, dtype=np.float32), heads], axis=1),
        "w1t": a["L0_attn_W1"].T,
        "w2t": a["L0_attn_W2"].T.reshape(MH, P, D).transpose(1, 0, 2),
        "w_att": np.stack([a["L0_attn_" + n].T for n in ("Wk", "Wv", "Wq", "Wo")], axis=1),
        "wgt": a["L0_ffn_w_gate"].T, "wut": a["L0_ffn_w_up"].T,
        "wdt": a["L0_ffn_w_down"].T.reshape(NM, P, D).transpose(1, 0, 2).reshape(P, NM * D),
    }
    nc = _bacc.Bacc("TRN2", target_bir_lowering=False, num_devices=1)
    arrays, args = {}, []
    for name in _NAMES:
        v = np.ascontiguousarray(lay[name])
        arrays[f"{name}_dram"] = v
        args.append(nc.dram_tensor(f"{name}_dram", v.shape, mybir.dt.from_np(v.dtype), kind="ExternalInput").ap())
    out = nc.dram_tensor("out_dram", (T, D), F32, kind="ExternalOutput").ap()
    build(nc, *args, out)
    r = _run(nc, [arrays], core_ids=[0])
    return r.results[0]["out_dram"].reshape(1, T, D)
```

```python
from contextlib import ExitStack

import numpy as np

import concourse.bass as bass
from concourse import mybir

F32, BF16, I32 = mybir.dt.float32, mybir.dt.bfloat16, mybir.dt.int32
ALU = mybir.AluOpType
ACT = mybir.ActivationFunctionType
AX = mybir.AxisListType

T, D, H = 2048, 128, 16
DH = D // H
P = 128
NT = T // P
BT = 512
NB = T // BT
TPB = BT // P
GH = 4
NG = H // GH
VW = 2 * DH
PARTS = 3
SHIFT_ROW = 96
HID = 384
NM = HID // P
MH = 2 * D // P
STEPS = NG * NT
EPS, LN_EPS = 1e-6, 1e-5
FFN_SCALE = 1.0 / 127.0
HEADROOM = 48.0
ARENA = 40 * 256
SUM_FLOOR = 2.0 ** -86
BIG = 1.0e38

AT_WO, AT_TR, AT_GATE, AT_UP, AT_DOWN = 7, 14, (18, 22, 27), (20, 25, 30), (36, 38, 40, 42)
M1_BANK, M2_BANK, NQ_BANK = ((2, 3), (4, 5), (6, 7), (7, 6)), (6, 7, 6, 7), (2, 3, 4, 5)
DOWN_BANK = (0, 3, 6, 7)
ONE_PAIR = float(np.array([0x3F803F80], np.uint32).view(np.float32)[0])


class Chain:

    def __init__(self, eng, sem, start=0):
        self.eng, self.sem, self.start, self.n = eng, sem, start, 0

    def did(self, ins):
        ins.then_inc(self.sem, 1)
        self.n += 1

    def after(self):
        self.eng.wait_ge(self.sem, self.start + self.n)


def build(nc, x, columns, wmod, fixed, w1t, w2t, w_att, wgt, wut, wdt, out):
    with ExitStack() as ctx:
        def sb(name, shape, dt=F32):
            return ctx.enter_context(nc.sbuf_tensor(name, shape, dt))

        def sem(name):
            return ctx.enter_context(nc.semaphore(name))

        q_scr = nc.dram_tensor("q_scr", (PARTS, D, T), BF16, kind="Internal").ap()
        k_scr = nc.dram_tensor("k_scr", (H, PARTS, DH, T), BF16, kind="Internal").ap()
        shift_scr = nc.dram_tensor("shift_scr", (H, PARTS, T), BF16, kind="Internal").ap()

        w1_sb = sb("w1_sb", [P, MH * P])
        w2_sb = sb("w2_sb", [P, MH, D])
        w_att_sb = sb("w_att_sb", [P, 4, D])
        wk_sb, wv_sb, wq_sb, wo_sb = (w_att_sb[:, i, :] for i in range(4))
        wmod_sb = sb("wmod_sb", [P, 6 * D])
        mod = sb("mod", [P, 6 * D])
        fixed_sb = sb("fixed_sb", [P, P + H + 64])
        ident_sb = fixed_sb[:, 0:P]
        hs_sb = fixed_sb[:, P:P + H]
        ones_bf = sb("ones_bf", [P, T], BF16)
        cols = sb("cols", [P, 8])
        b1_c, b2_c, eta_c, mmu_c, c_c, eta_s = cols[:, 0:2], cols[:, 2:3], cols[:, 3:4], cols[:, 4:5], cols[:, 5:6], \
            cols[:, 6:7]
        place_num, place_den = fixed_sb[:, P + H:P + H + 32], fixed_sb[:, P + H + 32:P + H + 64]
        hs_bf = sb("hs_bf", [P, H], BF16)
        silu_c = sb("silu_c", [P, 2])
        silu_b = sb("silu_b", [P, P])
        half = sb("half", [P, NT])
        mhalf = sb("mhalf", [P, NT])
        wg_f, wu_f = sb("wg_f", [P, HID]), sb("wu_f", [P, HID])
        wd_f = sb("wd_f", [P, NM, D])

        x_tm = sb("x_tm", [P, NT, D])
        K_op = sb("K_op", [P, H, T], BF16)
        Q_op = sb("Q_op", [P, 2 * H * BT], BF16)
        V_op = sb("V_op", [P, NT, H * VW + VW])
        probs = sb("probs", [P, 4, 2 * BT])
        O_sb = sb("O_sb", [P, NG, BT])

        arena = sb("arena", [P, ARENA])
        at = [0]

        def tmp(words, *shape, dt=F32):
            v = arena[:, at[0]:at[0] + words]
            at[0] += words
            assert at[0] <= ARENA
            if dt != F32:
                v = v.bitcast(dt)
            if len(shape) == 2:
                v = v.rearrange("p (a b) -> p a b", a=shape[0])
            return v

        num_T = tmp(BT)
        den_T = tmp(BT)
        over = at[0]
        h_tm = tmp(NT * D, NT, D)
        sp_tm = tmp(NT * D, NT, D)
        g_fm = tmp(NB * BT, NB, BT)
        q_parts = [tmp(PARTS * BT // 2, PARTS, BT, dt=BF16) for _ in range(3)]
        shift_f = [O_sb[0:H, b, :] for b in range(NB)]
        shift_bf = [w[0:H, BT // 2 * i:BT // 2 * (i + 1)].bitcast(BF16)
                    for w, i in ((wmod_sb, 0), (wmod_sb, 1), (wmod_sb, 2), (w1_sb, 0))]
        shift_parts = tmp(PARTS * BT // 2, PARTS, BT, dt=BF16)[0:H, :, :]
        vT = h_tm.rearrange("p (b a) d -> p b (a d)", b=NB)
        spare_sp = sp_tm.rearrange("p (b a) d -> p b (a d)", b=NB)
        rqs = [spare_sp[:, b, :] for b in range(NB)]
        sqqs = [v[:, BT // 2 * i:BT // 2 * (i + 1)].bitcast(BF16) for v in (num_T, den_T) for i in range(2)]
        second = Q_op[:, H * BT:2 * H * BT].bitcast(F32)
        hT = second[:, 0:NB * BT].rearrange("p (a b) -> p a b", a=NB)
        m1s = second[:, NB * BT:NB * BT + 2 * MH * BT].rearrange("p (a m b) -> p a m b", a=2, m=MH)
        k_parts = [probs[:, i, 0:PARTS * BT // 2].bitcast(BF16).rearrange("p (a b) -> p a b", a=PARTS)
                   for i in range(2)] + [q_parts[2]]
        rks = [probs[:, 2, 0:BT], probs[:, 2, BT:2 * BT]]
        sqks = [probs[:, 3, BT // 2 * b:BT // 2 * (b + 1)].bitcast(BF16) for b in range(NB)]
        junk2 = probs[:, 3, BT:2 * BT]
        wg_i, wu_i = wg_f[:, :].bitcast(I32), wu_f[:, :].bitcast(I32)
        wd_i = wd_f[:, :, :].rearrange("p a b -> p (a b)").bitcast(I32)
        at[0] = over
        rec_T = tmp(BT)
        att_T = tmp(BT)
        junk = tmp(BT)
        x1 = tmp(BT, TPB, D)
        sp1 = tmp(BT, TPB, D)
        sq1 = tmp(BT, TPB, D)
        h2 = tmp(BT, TPB, D)
        h2_T = tmp(BT)
        th = [tmp(BT) for _ in range(NM)]
        gl = [tmp(BT) for _ in range(NM)]
        hid = tmp(NM * BT, NM, BT)
        y = tmp(BT, TPB, D)
        stat = sb("stat", [P, NT, 6])
        mv = sb("mv", [P, NT, 2])
        small = sb("small", [P, 16, NT])
        (rstd, n2, a2, y0, yc, t1, t2, rt, u, ln_u, nmr, dv0, inn, dn, fac, spare) = \
            (small[:, i, :] for i in range(16))
        kmax = sb("kmax", [P, 8])
        ok = sb("ok", [P, 3, NB])
        flag_f = sb("flag_f", [P, 4])
        flag_i = sb("flag_i", [P, 2], I32)
        mx = sb("mx", [P, TPB, H])

        ps = ctx.enter_context(nc.psum_tensor("ps", [P, 8, 512], F32))

        def bank(i):
            return ps[:, i, :]

        def slot_bank(s):
            return ps[:, 2 * s:2 * s + 2, :]

        O_bank, M_bank = bank(6), bank(7)

        names = """c_in wmod_in w_in hs_ready ffn_in const_ready pe_mod mod_ready silu_ready ffn_ready
        vec root_in root_out stat_ready xn_done h_scaled ln_in ln_out h_ready v_ready
        hT_ps hT_sb m1_ps m1_sb m2_ps m2_sb vT_ps vT_sb k_ps q_ps v_ps
        k_hi k_res k_mid k_lo q_f q_hi q_res q_mid q_lo k_sq q_sq nk_ps nk_done nq_ps
        v_done kmax_ready bound shift_ready K_filled Q_filled Q_loaded ones_ready
        scores exped pv_done o_evac norm wo_ps h2_done h2T_ps h2T_done gate_ps up_ps gate_th
        gated glu_done down_ps y_ready y_stored tail epow_in epow_out flag_in flag_ps flag_ready placed exp_table warm num_in den_in
        max_loaded shift_saved max_zero max_scores max_taken max_T""".split()
        S = {n: sem(n) for n in names}
        k_st = [[sem(f"k_st{i}{n}") for n in range(PARTS)] for i in range(3)]
        q_st = [sem(f"q_st{b}") for b in range(NB)]
        x_in = [sem(f"x_in{b}") for b in range(NB)]
        o_in = [sem(f"o_in{g}") for g in range(NG)]
        K_loaded = [sem(f"K_loaded{g}") for g in range(NG)]

        def q_slot(s):
            return lambda h: Q_op[:, bass.ds(s * (H * BT) + h * BT, BT)]

        def row3(m, n):
            return mod[:, D * m:D * (m + 1)].unsqueeze(1).to_broadcast([P, n, D])

        block = ctx.enter_context(nc.Block())
        QUERY_LOADS = PARTS * PARTS + 1

        @block.sync
        def _(sp):
            xt = x.rearrange("(t p) d -> p t d", p=P)
            for b in range(NB):
                sp.dma_start(x_tm[:, TPB * b:TPB * (b + 1), :], xt[:, TPB * b:TPB * (b + 1), :]).then_inc(x_in[b], 16)

            for dst, src in ((fixed_sb[:, :], fixed), (w1_sb[:, :], w1t), (w2_sb[:, :, :], w2t),
                             (w_att_sb[:, :, :], w_att)):
                sp.dma_start(dst, src).then_inc(S["w_in"], 16)
            for dst, src in ((wg_i, wgt), (wu_i, wut), (wd_i, wdt)):
                sp.dma_start(dst, src).then_inc(S["ffn_in"], 16)

            def store_k(b):
                for n, part in enumerate(("k_hi", "k_mid", "k_lo")):
                    sp.wait_ge(S[part], b + 1)
                    sp.dma_start(k_scr[:, n, :, b * BT:(b + 1) * BT], k_parts[b % 3][:, n, :])\
                        .then_inc(k_st[b % 3][n], 16)

            def load_k(g):
                src = k_scr[GH * g:GH * (g + 1), :, :, :].rearrange("h a i t -> (a i) h t")
                for a in range(PARTS):
                    sp.dma_start(K_op[PARTS * DH * a:PARTS * DH * (a + 1), GH * g:GH * (g + 1), :], src)\
                        .then_inc(K_loaded[g], 16)

            def load_q(slot, b, loaded):
                q3 = Q_op[:, slot * H * BT:(slot + 1) * H * BT].rearrange("p (h t) -> p h t", h=H)
                tb = slice(b * BT, (b + 1) * BT)
                for s in range(PARTS * PARTS):
                    src = q_scr[s // PARTS, :, tb].rearrange("(h i) t -> i h t", i=DH)
                    sp.dma_start(q3[DH * s:DH * (s + 1), :, :], src).then_inc(loaded, 16)

            def load_shift(slot, b, loaded, p):
                q3 = Q_op[:, slot * H * BT:(slot + 1) * H * BT].rearrange("p (h t) -> p h t", h=H)
                if p:
                    sp.dma_start(q3[SHIFT_ROW:SHIFT_ROW + PARTS, :, :],
                                 shift_scr[:, :, b * BT:(b + 1) * BT].rearrange("h a t -> a h t")).then_inc(loaded, 16)
                else:
                    sp.dma_start(q3[SHIFT_ROW:SHIFT_ROW + 1, :, :], shift_bf[b]).then_inc(loaded, 16)

            for b in range(NB):
                store_k(b)
            sp.wait_ge(S["K_filled"], 2)
            for i in range(3):
                for n in range(PARTS):
                    sp.wait_ge(k_st[i][n], 16 * len(range(i, NB, 3)))
            load_k(0)
            sp.wait_ge(S["q_lo"], 1)
            sp.dma_start(q_scr[:, :, 0:BT].rearrange("a f t -> f a t"), q_parts[0]).then_inc(q_st[0], 16)
            sp.wait_ge(q_st[0], 16)
            sp.wait_ge(S["Q_filled"], 1)
            load_q(0, 0, S["Q_loaded"])
            sp.wait_ge(S["shift_ready"], 1)
            load_shift(0, 0, S["Q_loaded"], 0)
            for g in range(1, NG):
                sp.wait_ge(S["K_filled"], 2 * (g + 1))
                load_k(g)

            def gather(Bk, g):
                sp.wait_ge(S["o_evac"], NG * Bk + g + 1)
                if Bk % NB and g == 0:
                    sp.wait_ge(S["norm"], Bk)
                for j in range(GH):
                    rows = slice(GH * DH * g + DH * j, GH * DH * g + DH * (j + 1))
                    sp.dma_start(num_T[rows, :], O_sb[32 * j:32 * j + DH, g, :]).then_inc(o_in[g], 16)
                    sp.dma_start(den_T[rows, :], O_sb[32 * j + DH:32 * j + 2 * DH, g, :]).then_inc(o_in[g], 16)

            ot = out.rearrange("(t p) d -> p t d", p=P)

            def store(Bk):
                b = Bk % NB
                sp.wait_ge(S["y_ready"], Bk + 1)
                sp.dma_start(ot[:, TPB * b:TPB * (b + 1), :], y).then_inc(S["y_stored"], 16)

            def blocks(p):
                for b in range(NB):
                    Bk = NB * p + b
                    if b:
                        gather(Bk - 1, NG - 1)
                    if b + 1 < NB:
                        if not p:
                            sp.wait_ge(q_st[b + 1], 16)
                            sp.wait_ge(S["shift_ready"], b + 2)
                            sp.wait_ge(S["Q_filled"], 2)
                        sp.wait_ge(S["Q_loaded"], 16 * QUERY_LOADS * (Bk + 1))
                        if Bk:
                            sp.wait_ge(S["scores"], 2 * STEPS * Bk)
                        load_q((b + 1) % 2, b + 1, S["Q_loaded"])
                        load_shift((b + 1) % 2, b + 1, S["Q_loaded"], p)
                    for g in range(NG - 1):
                        gather(Bk, g)
                        if b and g == 1:
                            store(Bk - 1)
                store(NB * (p + 1) - 1)
                sp.wait_ge(S["y_stored"], 16 * NB * (p + 1) + 1)

            blocks(0)

            sp.wait_ge(S["flag_ready"], 1)
            with sp.If(sp.value_load(flag_i[0:1, 0:1], min_val=0, max_val=1)):
                sp.wait_ge(S["max_zero"], 1)
                for b in range(NB):
                    sp.wait_ge(S["max_taken"], NT * GH * b + 1)
                    load_q(0, b, S["max_loaded"])
                    sp.wait_ge(S["max_loaded"], 16 * PARTS * PARTS * (b + 1))
                    sp.wait_ge(S["shift_ready"], NB + b + 1)
                    sp.dma_start(shift_scr[:, :, b * BT:(b + 1) * BT], shift_parts).then_inc(S["shift_saved"], 16)
                    sp.wait_ge(S["shift_saved"], 16 * (b + 1))
                load_q(0, 0, S["Q_loaded"])
                load_shift(0, 0, S["Q_loaded"], 1)
                blocks(1)

        @block.gpsimd
        def _(pool):
            pool.memset(half[:, :], 0.5).then_inc(S["const_ready"], 1)
            pool.memset(mhalf[:, :], -0.5).then_inc(S["const_ready"], 1)
            pool.memset(V_op[:, :, :], 1.0).then_inc(S["ones_ready"], 1)
            pool.wait_ge(S["const_ready"], 2)

            def root(dst, src, power, n, asked, done):
                pool.wait_ge(S[asked], n)
                pool.tensor_tensor(dst, src, power, ALU.pow).then_inc(S[done], 1)
                pool.wait_ge(S[done], n)

            def fill_k(g):
                hg = slice(GH * g, GH * (g + 1))
                pool.memset(K_op[64:96, hg, :].bitcast(F32), 0.0).then_inc(S["K_filled"], 1)
                pool.wait_ge(S["K_filled"], 2 * g + 1)
                pool.memset(K_op[96:128, hg, :].bitcast(F32), ONE_PAIR).then_inc(S["K_filled"], 1)
                pool.wait_ge(S["K_filled"], 2 * g + 2)

            pool.wait_ge(S["ones_ready"], 1)
            fill_k(0)
            for b in range(NB):
                hb = h_tm[:, TPB * b:TPB * (b + 1), :]
                pool.wait_ge(S["h_scaled"], b + 1)
                pool.tensor_tensor(hb, hb, row3(0, TPB), ALU.add).then_inc(S["h_ready"], 1)
                pool.wait_ge(S["h_ready"], b + 1)
            pool.memset(Q_op[64:128, 0:H * BT].bitcast(F32), 0.0).then_inc(S["Q_filled"], 1)
            pool.wait_ge(S["Q_filled"], 1)
            pool.wait_ge(S["w_in"], 16 * 4)
            pool.tensor_copy(hs_bf[:, :], hs_sb).then_inc(S["hs_ready"], 1)
            pool.wait_ge(S["hs_ready"], 1)
            for g in range(1, NG):
                fill_k(g)
            for b in range(1, NB):
                pool.wait_ge(S["q_lo"], b + 1)
                pool.dma_start(q_scr[:, :, b * BT:(b + 1) * BT].rearrange("a f t -> f a t"), q_parts[b % 3])\
                    .then_inc(q_st[b], 16)
            pool.wait_ge(S["m2_ps"], NB)
            pool.memset(Q_op[64:128, H * BT:2 * H * BT].bitcast(F32), 0.0).then_inc(S["Q_filled"], 1)
            pool.wait_ge(S["Q_filled"], 2)
            def tail_roots(Bk):
                r4 = slice(0, TPB)
                root(small[:, 1, r4], small[:, 2, r4], half[:, r4], 2 * Bk + 1, "epow_in", "epow_out")
                root(small[:, 3, r4], small[:, 4, r4], mhalf[:, r4], 2 * Bk + 2, "epow_in", "epow_out")

            with pool.Fori(0, NB) as b:
                tail_roots(b)

            pool.wait_ge(S["flag_ready"], 1)
            with pool.If(pool.value_load(flag_i[0:1, 0:1], min_val=0, max_val=1)):
                pool.memset(Q_op[96:128, 0:H * BT].bitcast(F32), 0.0).then_inc(S["max_zero"], 1)
                with pool.Fori(NB, 2 * NB) as b:
                    tail_roots(b)

        @block.scalar
        def _(act):
            act.dma_start(cols[:, 0:6], columns).then_inc(S["c_in"], 16)
            act.dma_start(wmod_sb[:, :], wmod).then_inc(S["wmod_in"], 16)
            act.wait_ge(S["c_in"], 16)
            act.activation(silu_c[:, 0:1], c_c, ACT.Exp, scale=-1.0).then_inc(S["silu_ready"], 1)

            def copy_hT(b):
                act.wait_ge(S["hT_ps"], b + 1)
                act.activation(hT[:, b, :], bank(b % 2), ACT.Identity, bias=mmu_c).then_inc(S["hT_sb"], 1)

            def tanh1(b):
                for m in range(MH):
                    act.wait_ge(S["m1_ps"], MH * b + m + 1)
                    if b >= 2:
                        act.wait_ge(S["m2_ps"], b - 1)
                    act.activation(m1s[:, b % 2, m, :], bank(M1_BANK[b][m]), ACT.Tanh, bias=b1_c[:, m:m + 1]).then_inc(S["m1_sb"], 1)

            def tanh2(b):
                act.wait_ge(S["m2_ps"], b + 1)
                act.activation(g_fm[:, b, :], bank(M2_BANK[b]), ACT.Tanh, bias=b2_c).then_inc(S["m2_sb"], 1)

            def root(dst, src, n):
                act.wait_ge(S["root_in"], n)
                act.activation(dst, src, ACT.Sqrt).then_inc(S["root_out"], 1)

            root(rt, spare, 1)
            act.wait_ge(S["stat_ready"], 1)
            for t in range(NT):
                act.activation(h_tm[:, t, :], x_tm[:, t, :], ACT.Identity, scale=rstd[:, t:t + 1],
                               bias=nmr[:, t:t + 1]).then_inc(S["xn_done"], 1)
            for b in range(NB):
                copy_hT(b)
            root(y0, a2, 2)
            root(rt, t2, 3)
            root(dn, inn, 4)
            act.wait_ge(S["ln_in"], 1)
            act.activation(ln_u, u, ACT.Ln).then_inc(S["ln_out"], 1)

            def copy_vT(b):
                act.wait_ge(S["vT_ps"], b + 1)
                act.activation(vT[:, b, :], bank(b % 2), ACT.Identity).then_inc(S["vT_sb"], 1)

            def k_split1(b):
                act.wait_ge(S["k_ps"], b + 1)
                if b == 3:
                    for n in range(PARTS):
                        act.wait_ge(k_st[0][n], 16)
                act.activation(k_parts[b % 3][:, 0, :], bank(2 + b % 2), ACT.Identity).then_inc(S["k_hi"], 1)
                act.activation(sqks[b], bank(2 + b % 2), ACT.Square).then_inc(S["k_sq"], 1)

            def k_split2(b):
                act.wait_ge(S["k_res"], b + 1)
                act.activation(k_parts[b % 3][:, 1, :], rks[b % 2], ACT.Identity).then_inc(S["k_mid"], 1)

            def q_split1(b):
                act.wait_ge(S["q_f"], b + 1)
                if b == 2:
                    for n in range(PARTS):
                        act.wait_ge(k_st[2][n], 16)
                if b == 3:
                    act.wait_ge(q_st[0], 16)
                act.activation(q_parts[b % 3][:, 0, :], g_fm[:, b, :], ACT.Identity).then_inc(S["q_hi"], 1)
                act.activation(sqqs[b], g_fm[:, b, :], ACT.Square).then_inc(S["q_sq"], 1)

            def q_split2(b):
                act.wait_ge(S["q_res"], b + 1)
                act.activation(q_parts[b % 3][:, 1, :], rqs[b], ACT.Identity).then_inc(S["q_mid"], 1)

            def bound(b):
                act.wait_ge(S["nq_ps"], b + 1)
                act.wait_ge(S["kmax_ready"], 1)
                act.activation(shift_f[b], bank(NQ_BANK[b])[0:H, :], ACT.Sqrt, scale=kmax[0:H, NB:NB + 1])\
                    .then_inc(S["bound"], 1)

            tanh1(0)
            copy_vT(0)
            copy_vT(1)
            k_split1(0)
            tanh1(1)
            k_split2(0)
            tanh2(0)
            k_split1(1)
            copy_vT(2)
            k_split2(1)
            copy_vT(3)
            tanh2(1)
            k_split1(2)
            tanh1(2)
            k_split2(2)
            k_split1(3)
            tanh2(2)
            k_split2(3)
            q_split1(0)
            q_split2(0)
            tanh1(3)
            tanh2(3)
            q_split1(1)
            bound(0)
            q_split1(2)
            q_split2(1)
            q_split1(3)
            q_split2(2)
            q_split2(3)
            for b in range(1, NB):
                bound(b)
            act.activation(silu_c[:, 1:2], c_c, ACT.Exp).then_inc(S["exp_table"], 1)
            act.wait_ge(S["q_lo"], NB)

            def block_steps(Bk, tails):
                for j in range(STEPS):
                    for half_ in range(2):
                        u = 2 * j + half_
                        act.wait_ge(S["scores"], Bk * 2 * STEPS + u + 1)
                        act.activation(probs[:, 2 * (j % 2) + half_, :], slot_bank(u % 3), ACT.Exp)\
                            .then_inc(S["exped"], 1)
                    if tails:
                        if j == AT_TR:
                            copy_h2(Bk - 1)
                        if j in AT_GATE:
                            gate(Bk - 1, AT_GATE.index(j), M_bank)

            def copy_h2(Bk):
                act.wait_ge(S["h2T_ps"], Bk + 1)
                act.activation(h2_T, M_bank, ACT.Identity).then_inc(S["h2T_done"], 1)

            def gate(Bk, m, from_bank):
                act.wait_ge(S["gate_ps"], Bk * NM + m + 1)
                act.activation(th[m], from_bank, ACT.Tanh, scale=0.5).then_inc(S["gate_th"], 1)

            def blocks(p):
                block_steps(NB * p, False)
                with act.Fori(NB * p + 1, NB * (p + 1)) as Bk:
                    block_steps(Bk, True)
                last = NB * (p + 1) - 1
                act.wait_ge(S["placed"], p + 1)
                act.activation(num_T[96:128, :], bank(0)[96:128, :], ACT.Identity).then_inc(S["num_in"], 1)
                act.activation(den_T[96:128, :], bank(1)[96:128, :], ACT.Identity).then_inc(S["den_in"], 1)
                copy_h2(last)
                for m in range(NM):
                    gate(last, m, bank(m))

            blocks(0)
            act.wait_ge(S["flag_ready"], 1)
            with act.If(act.value_load(flag_i[0:1, 0:1], min_val=0, max_val=1)):
                blocks(1)

        @block.tensor
        def _(pe):
            pe.wait_ge(S["mod_ready"], 1)
            pe.wait_ge(S["wmod_in"], 16)
            for i in range(2):
                ins = pe.matmul(bank(6 + i)[:, 0:3 * D], silu_b[:, :], wmod_sb[:, 3 * D * i:3 * D * (i + 1)],
                                start=True, stop=True)
            ins.then_inc(S["pe_mod"], 1)
            pe.wait_ge(S["w_in"], 16 * 4)

            def transposes(src, b, done):
                for t in range(TPB):
                    ins = pe.transpose(bank(b % 2)[:, P * t:P * (t + 1)], src[:, TPB * b + t, :], ident_sb)
                ins.then_inc(S[done], 1)

            def metric_T(b):
                pe.wait_ge(S["h_ready"], b + 1)
                if b >= 2:
                    pe.wait_ge(S["hT_sb"], b - 1)
                transposes(h_tm, b, "hT_ps")

            def metric(b):
                pe.wait_ge(S["hT_sb"], b + 1)
                for m in range(MH):
                    if b == 2:
                        pe.wait_ge(S["m2_sb"], m + 1)
                    if b == 3:
                        pe.wait_ge(*((S["m1_sb"], MH * b) if m == 0 else (S["m2_sb"], b)))
                    pe.matmul(bank(M1_BANK[b][m]), w1_sb[:, P * m:P * (m + 1)], hT[:, b, :], start=True, stop=True)\
                        .then_inc(S["m1_ps"], 1)

            def metric2(b):
                pe.wait_ge(S["m1_sb"], MH * (b + 1))
                for m in range(MH):
                    ins = pe.matmul(bank(M2_BANK[b]), w2_sb[:, m, :], m1s[:, b % 2, m, :],
                                    start=m == 0, stop=m == MH - 1)
                ins.then_inc(S["m2_ps"], 1)

            for b in range(NB):
                metric_T(b)
            metric(0)
            metric(1)

            def v_T(b):
                pe.wait_ge(S["v_ready"], b + 1)
                pe.wait_ge(S["hT_sb"], NB)
                if b >= 2:
                    pe.wait_ge(S["vT_sb"], b - 1)
                transposes(sp_tm, b, "vT_ps")

            def k_of(b):
                pe.wait_ge(S["vT_sb"], b + 1)
                if b >= 2:
                    pe.wait_ge(S["k_res"], b - 1)
                pe.matmul(bank(2 + b % 2), wk_sb, vT[:, b, :], start=True, stop=True).then_inc(S["k_ps"], 1)

            def v_of(b):
                if b >= 2:
                    pe.wait_ge(S["v_done"], b - 1)
                for t in range(TPB):
                    ins = pe.matmul(bank(4 + b % 2)[:, P * t:P * (t + 1)], vT[:, b, P * t:P * (t + 1)], wv_sb,
                                    start=True, stop=True)
                ins.then_inc(S["v_ps"], 1)

            def nk(b):
                pe.wait_ge(S["k_sq"], b + 1)
                if b:
                    pe.wait_ge(S["nk_done"], b)
                pe.matmul(bank(0)[0:H, :], hs_bf[:, :], sqks[b], start=True, stop=True).then_inc(S["nk_ps"], 1)

            def q_of(b):
                if b:
                    pe.wait_ge(S["q_f"], b)
                pe.matmul(bank(1), wq_sb, vT[:, b, :], start=True, stop=True).then_inc(S["q_ps"], 1)

            def nq(b):
                pe.wait_ge(S["q_sq"], b + 1)
                pe.matmul(bank(NQ_BANK[b])[0:H, :], hs_bf[:, :], sqqs[b], start=True, stop=True).then_inc(S["nq_ps"], 1)

            v_T(0)
            v_T(1)
            k_of(0)
            metric2(0)
            pe.wait_ge(S["m1_sb"], MH * 2)
            v_of(0)
            k_of(1)
            v_of(1)
            metric2(1)
            v_T(2)
            v_T(3)
            k_of(2)
            v_of(2)
            metric(2)
            k_of(3)
            v_of(3)
            metric2(2)
            pe.wait_ge(S["vT_sb"], NB)
            pe.wait_ge(S["hs_ready"], 1)
            nk(0)
            q_of(0)
            nk(1)
            metric(3)
            nk(2)
            q_of(1)
            nk(3)
            pe.wait_ge(S["k_res"], NB)
            pe.wait_ge(S["v_done"], NB)
            nq(0)
            metric2(3)
            for b in range(2, NB):
                q_of(b)
            for b in range(1, NB):
                nq(b)

            def keep_warm(n, to):
                for _ in range(n):
                    ins = pe.matmul(to, ones_bf[:, 0:P], ones_bf[:, 0:BT], start=True, stop=True)
                ins.then_inc(S["warm"], 1)

            def score(Bk, j):
                start = isinstance(Bk, int) and Bk == 0
                g, kt = divmod(j, NT)
                if kt == 0 and start:
                    pe.wait_ge(K_loaded[g], 16 * PARTS)
                queries = q_slot(Bk % 2)
                for half_ in range(2):
                    u = 2 * j + half_
                    if u >= 3:
                        pe.wait_ge(S["exped"], Bk * 2 * STEPS + u - 2)
                    elif u < 2 and not start:
                        pe.wait_ge(S["exped"], Bk * 2 * STEPS + u - 1)
                    for i in range(2):
                        h = GH * g + 2 * half_ + i
                        ins = pe.matmul(slot_bank(u % 3)[:, i, :], K_op[:, h, P * kt:P * (kt + 1)], queries(h),
                                        start=True, stop=True)
                    ins.then_inc(S["scores"], 1)

            def product(Bk, j):
                g, kt = divmod(j, NT)
                pe.wait_ge(S["exped"], Bk * 2 * STEPS + 2 * j + 2)
                if kt == 0 and not (isinstance(Bk, int) and Bk == 0 and g == 0):
                    pe.wait_ge(S["o_evac"], Bk * NG + g)
                for i in range(GH):
                    h = GH * g + i
                    ins = pe.matmul(O_bank[32 * i:32 * (i + 1), :], V_op[:, kt, VW * h:VW * h + 32],
                                    probs[:, 2 * (j % 2) + i // 2, BT * (i % 2):BT * (i % 2 + 1)],
                                    start=kt == 0, stop=kt == NT - 1, tile_position=(0, 32 * i))
                if kt == NT - 1:
                    ins.then_inc(S["pv_done"], 1)

            def t_wo(Bk):
                pe.wait_ge(S["norm"], Bk + 1)
                for t in range(TPB):
                    ins = pe.matmul(M_bank[:, P * t:P * (t + 1)], att_T[:, P * t:P * (t + 1)], wo_sb,
                                    start=True, stop=True)
                ins.then_inc(S["wo_ps"], 1)

            def t_transpose(Bk):
                pe.wait_ge(S["h2_done"], Bk + 1)
                for t in range(TPB):
                    ins = pe.transpose(M_bank[:, P * t:P * (t + 1)], h2[:, t, :], ident_sb)
                ins.then_inc(S["h2T_ps"], 1)

            def t_gate(Bk, m, to):
                pe.wait_ge(S["h2T_done"], Bk + 1)
                if m and to is M_bank:
                    pe.wait_ge(S["glu_done"], Bk * NM + m)
                pe.matmul(to, wg_f[:, P * m:P * (m + 1)], h2_T, start=True, stop=True).then_inc(S["gate_ps"], 1)

            def t_up(Bk, m, to):
                if to is M_bank:
                    pe.wait_ge(S["gated"], Bk * NM + m + 1)
                pe.matmul(to, wu_f[:, P * m:P * (m + 1)], h2_T, start=True, stop=True).then_inc(S["up_ps"], 1)

            def t_down(Bk, to, tiles=range(TPB)):
                if tiles[0] == 0:
                    pe.wait_ge(S["glu_done"], Bk * NM + NM)
                for t in tiles:
                    for m in range(NM):
                        ins = pe.matmul(to[:, P * t:P * (t + 1)], hid[:, m, P * t:P * (t + 1)], wd_f[:, m, :],
                                        start=m == 0, stop=m == NM - 1)
                if tiles[-1] == TPB - 1:
                    ins.then_inc(S["down_ps"], 1)

            def block_steps(Bk, tails):
                for j in range(STEPS):
                    score(Bk, j)
                    if j:
                        product(Bk, j - 1)
                    elif tails:
                        product(Bk - 1, STEPS - 1)
                    if tails:
                        if j == AT_WO:
                            t_wo(Bk - 1)
                        if j == AT_TR:
                            t_transpose(Bk - 1)
                        if j in AT_GATE:
                            t_gate(Bk - 1, AT_GATE.index(j), M_bank)
                        if j in AT_UP:
                            t_up(Bk - 1, AT_UP.index(j), M_bank)
                        if j in AT_DOWN:
                            t_down(Bk - 1, M_bank, [AT_DOWN.index(j)])

            def blocks(p):
                first, last = NB * p, NB * (p + 1) - 1
                pe.wait_ge(S["Q_loaded"], 16 * QUERY_LOADS * (first + 1))
                block_steps(first, False)
                if p == 0:
                    pe.wait_ge(S["ffn_ready"], 3)
                with pe.Fori(first + 1, last + 1) as Bk:
                    pe.wait_ge(S["Q_loaded"], 16 * QUERY_LOADS * (Bk + 1))
                    block_steps(Bk, True)
                product(last, STEPS - 1)
                pe.wait_ge(S["o_evac"], NG * (last + 1))
                pe.matmul(bank(0)[96:128, :], place_num, O_sb[:, NG - 1, :], start=True, stop=True,
                          tile_position=(0, 96))
                pe.matmul(bank(1)[96:128, :], place_den, O_sb[:, NG - 1, :], start=True, stop=True,
                          tile_position=(0, 96)).then_inc(S["placed"], 1)
                t_wo(last)
                pe.wait_ge(S["epow_out"], 2 * (last + 1))
                keep_warm(7, bank(5))
                t_transpose(last)
                keep_warm(2, bank(5))
                for m in range(NM):
                    t_gate(last, m, bank(m))
                    t_up(last, m, bank(3 + m))
                for m in range(NM):
                    pe.wait_ge(S["glu_done"], last * NM + m + 1)
                    for t in range(TPB):
                        ins = pe.matmul(bank(DOWN_BANK[t])[:, P * t:P * (t + 1)], hid[:, m, P * t:P * (t + 1)], wd_f[:, m, :],
                                        start=m == 0, stop=m == NM - 1)
                ins.then_inc(S["down_ps"], 1)
                if p == 0:
                    pe.wait_ge(S["flag_in"], 1)
                    pe.matmul(bank(2)[0:1, 0:1], flag_f[:, 0:1], flag_f[:, 1:2], start=True, stop=True)\
                        .then_inc(S["flag_ps"], 1)

            pe.wait_ge(S["m2_sb"], NB)
            keep_warm(7, M_bank)
            for done in ("vT_sb", "k_res", "v_done", "nk_done", "q_f", "bound"):
                pe.wait_ge(S[done], NB)
            blocks(0)

            pe.wait_ge(S["flag_ready"], 1)
            with pe.If(pe.value_load(flag_i[0:1, 0:1], min_val=0, max_val=1)):
                q_all = q_slot(0)
                with pe.Fori(0, NB) as b:
                    pe.wait_ge(S["max_loaded"], 16 * PARTS * PARTS * (b + 1))
                    for h in range(H):
                        for t in range(TPB):
                            pe.wait_ge(S["max_taken"], b * (H * TPB) + h * TPB + t + 1)
                            for i in range(NB):
                                ins = pe.matmul(bank(i), q_all(h)[:, P * t:P * (t + 1)],
                                                K_op[:, h, BT * i:BT * (i + 1)], start=True, stop=True)
                            ins.then_inc(S["max_scores"], 1)
                    pe.wait_ge(S["max_taken"], (b + 1) * (H * TPB) + 1)
                    for t in range(TPB):
                        ins = pe.transpose(M_bank[0:H, P * t:P * (t + 1)], mx[:, t, :], ident_sb)
                    ins.then_inc(S["max_T"], 1)
                blocks(1)

        @block.vector
        def _(dve):
            vec = Chain(dve, S["vec"])

            def split_shift(c, sf, parts):
                c.after()
                c.did(dve.tensor_copy(parts[:, 0, :], sf))
                c.after()
                c.did(dve.tensor_tensor(sf, sf, parts[:, 0, :], ALU.subtract))
                c.after()
                c.did(dve.tensor_copy(parts[:, 1, :], sf))
                c.after()
                dve.tensor_tensor(parts[:, 2, :], sf, parts[:, 1, :], ALU.subtract).then_inc(S["shift_ready"], 1)

            def newton(dst, rough, a, tmp_):
                vec.did(dve.reciprocal(tmp_, rough))
                vec.after()
                vec.did(dve.scalar_tensor_tensor(tmp_, a, 0.5, tmp_, ALU.mult, ALU.mult))
                vec.after()
                vec.did(dve.scalar_tensor_tensor(dst, rough, 0.5, tmp_, ALU.mult, ALU.add))
                vec.after()

            vec.did(dve.memset(ones_bf[:, :], 1.0))
            vec.did(dve.memset(ok[:, :, :], 1.0))
            vec.did(dve.memset(flag_f[:, :], 1.0))
            for b in range(NB):
                dve.wait_ge(x_in[b], 16)
                for t in range(TPB * b, TPB * (b + 1)):
                    vec.did(dve.bn_stats(stat[:, t, :], x_tm[:, t, :]))
                if b == 1:
                    dve.wait_ge(S["silu_ready"], 1)
                    vec.did(dve.tensor_scalar(silu_c[:, 1:2], silu_c[:, 0:1], 1.0, None, ALU.add))
                    vec.after()
                    vec.did(dve.reciprocal(silu_c[:, 0:1], silu_c[:, 1:2]))
                    vec.after()
                    dve.tensor_scalar(silu_b[:, :], ones_bf[:, 0:P], silu_c[:, 0:1], c_c, ALU.mult, ALU.mult)\
                        .then_inc(S["mod_ready"], 1)
            vec.after()
            for t in range(NT):
                vec.did(dve.bn_aggr(mv[:, t, :], stat[:, t, :]))
            vec.after()
            dve.tensor_scalar(spare, mv[:, :, 1], LN_EPS, None, ALU.add).then_inc(S["root_in"], 1)
            dve.wait_ge(S["pe_mod"], 1)
            vec.did(dve.tensor_copy(mod[:, 0:3 * D], bank(6)[:, 0:3 * D]))
            vec.did(dve.tensor_copy(mod[:, 3 * D:6 * D], bank(7)[:, 0:3 * D]))
            vec.after()
            for m in (1, 4):
                vec.did(dve.tensor_scalar(mod[:, D * m:D * (m + 1)], mod[:, D * m:D * (m + 1)], 1.0, None, ALU.add))
            dve.wait_ge(S["root_out"], 1)
            newton(a2, rt, spare, t1)
            vec.did(dve.reciprocal(rstd, a2))
            vec.after()
            dve.scalar_tensor_tensor(nmr, mv[:, :, 0], -1.0, rstd, ALU.mult, ALU.mult).then_inc(S["stat_ready"], 1)
            for m in (2, 5):
                gate = mod[:, D * m:D * (m + 1)]
                sign, size = junk2[:, 0:P], junk2[:, P:2 * P]
                vec.did(dve.tensor_scalar(sign, gate, 0.0, 2.0, ALU.is_ge, ALU.mult))
                vec.did(dve.scalar_tensor_tensor(size, gate, -1.0, gate, ALU.mult, ALU.max))
                vec.after()
                vec.did(dve.tensor_scalar(sign, sign, -1.0, None, ALU.add))
                vec.after()
                vec.did(dve.scalar_tensor_tensor(gate, size, 0.25, sign, ALU.max, ALU.mult))
                vec.after()
            def scale_h(b):
                hb = h_tm[:, TPB * b:TPB * (b + 1), :]
                dve.wait_ge(S["xn_done"], TPB * (b + 1))
                dve.tensor_tensor(hb, hb, row3(1, TPB), ALU.mult).then_inc(S["h_scaled"], 1)

            scale_h(0)
            for b in range(NB):
                hb, spb = h_tm[:, TPB * b:TPB * (b + 1), :], sp_tm[:, TPB * b:TPB * (b + 1), :]
                if b + 1 < NB:
                    scale_h(b + 1)
                dve.wait_ge(S["h_ready"], b + 1)
                vec.did(dve.tensor_scalar(spb, hb, 8.0, -8.0, ALU.min, ALU.max))
                vec.after()
                for t in range(TPB * b, TPB * (b + 1)):
                    vec.did(dve.tensor_tensor_reduce(junk2[:, P * (t % TPB) + 1:P * (t % TPB + 1)],
                                                     sp_tm[:, t, 1:D], sp_tm[:, t, 1:D], 1.0, 0.0,
                                                     ALU.mult, ALU.add, n2[:, t:t + 1]))
            vec.after()
            dve.tensor_scalar(a2, n2, 1.0, EPS, ALU.add, ALU.add).then_inc(S["root_in"], 1)
            dve.wait_ge(S["root_out"], 2)
            newton(y0, y0, a2, t1)
            vec.did(dve.tensor_scalar(yc, y0, 1.0 + EPS, None, ALU.max))
            vec.after()
            vec.did(dve.tensor_scalar(t1, yc, -1.0, None, ALU.add))
            vec.after()
            dve.scalar_tensor_tensor(t2, yc, 1.0, t1, ALU.add, ALU.mult).then_inc(S["root_in"], 1)
            vec.did(dve.tensor_tensor(dv0, y0, yc, ALU.subtract))
            vec.after()
            dve.wait_ge(S["root_in"], 3)
            vec.did(dve.tensor_tensor(t1, dv0, dv0, ALU.mult))
            vec.after()
            vec.did(dve.tensor_tensor(t1, n2, t1, ALU.subtract))
            vec.after()
            dve.tensor_scalar(inn, t1, EPS, None, ALU.max).then_inc(S["root_in"], 1)
            dve.wait_ge(S["root_in"], 4)
            dve.wait_ge(S["root_out"], 3)
            newton(rt, rt, t2, t1)
            dve.tensor_tensor(u, yc, rt, ALU.add).then_inc(S["ln_in"], 1)
            dve.wait_ge(S["root_out"], 4)
            newton(dn, dn, inn, t1)
            vec.did(dve.tensor_scalar(t1, dn, EPS, None, ALU.add))
            vec.after()
            vec.did(dve.reciprocal(fac, t1))
            vec.after()
            dve.wait_ge(S["ln_out"], 1)
            vec.did(dve.scalar_tensor_tensor(fac, ln_u, 0.001, fac, ALU.max, ALU.mult))
            vec.after()
            vec.did(dve.tensor_tensor(sp_tm[:, :, 0], dv0, fac, ALU.mult))
            for b in range(NB):
                for t in range(TPB * b, TPB * (b + 1)):
                    ins = dve.tensor_scalar(sp_tm[:, t, 1:D], sp_tm[:, t, 1:D], fac[:, t:t + 1], None, ALU.mult)
                    if t % TPB < TPB - 1:
                        vec.did(ins)
                ins.then_inc(S["v_ready"], 1)

            def metric(b):
                dve.wait_ge(S["m2_sb"], b + 1)
                vec.did(dve.tensor_scalar(g_fm[:, b, :], g_fm[:, b, :], 0.1 * DH ** -0.5, eta_s, ALU.mult, ALU.add))

            def queries(b):
                vec.after()
                dve.wait_ge(S["q_ps"], b + 1)
                dve.tensor_tensor(g_fm[:, b, :], bank(1), g_fm[:, b, :], ALU.mult)\
                    .then_inc(S["q_f"], 1)

            def queries_rest(b):
                dve.wait_ge(S["q_hi"], b + 1)
                dve.wait_ge(S["q_f"], b + 1)
                dve.tensor_tensor(rqs[b], g_fm[:, b, :], q_parts[b % 3][:, 0, :], ALU.subtract)\
                    .then_inc(S["q_res"], 1)

            def queries_low(b):
                dve.wait_ge(S["q_mid"], b + 1)
                dve.wait_ge(S["q_res"], b + 1)
                dve.tensor_tensor(q_parts[b % 3][:, 2, :], rqs[b], q_parts[b % 3][:, 1, :], ALU.subtract)\
                    .then_inc(S["q_lo"], 1)

            def k_max(b):
                dve.wait_ge(S["nk_ps"], b + 1)
                dve.tensor_reduce(kmax[0:H, b:b + 1], bank(0)[0:H, :], AX.X, ALU.max).then_inc(S["nk_done"], 1)

            def shift(b):
                dve.wait_ge(S["bound"], b + 1)
                dve.tensor_scalar(shift_bf[b], shift_f[b], -1.0 - 2.0 ** -7, HEADROOM, ALU.mult, ALU.add)\
                    .then_inc(S["shift_ready"], 1)

            vec.did(dve.tensor_scalar(eta_s, eta_c, DH ** -0.5, None, ALU.mult))
            def k_rest(b):
                dve.wait_ge(S["k_sq"], b + 1)
                if b >= 2:
                    dve.wait_ge(S["k_mid"], b - 1)
                    dve.wait_ge(S["k_lo"], b - 1)
                dve.tensor_tensor(rks[b % 2], bank(2 + b % 2), k_parts[b % 3][:, 0, :], ALU.subtract)\
                    .then_inc(S["k_res"], 1)

            def k_low(b):
                dve.wait_ge(S["k_mid"], b + 1)
                dve.wait_ge(S["k_res"], b + 1)
                dve.tensor_tensor(k_parts[b % 3][:, 2, :], rks[b % 2], k_parts[b % 3][:, 1, :], ALU.subtract)\
                    .then_inc(S["k_lo"], 1)

            def values(b):
                dve.wait_ge(S["v_ps"], b + 1)
                for t in range(TPB):
                    ins = dve.tensor_copy(
                        V_op[:, TPB * b + t, 0:H * VW].rearrange("p (h w) -> p h w", h=H)[:, :, 0:DH],
                        bank(4 + b % 2)[:, P * t:P * (t + 1)].rearrange("p (h i) -> p h i", h=H))
                    if t < TPB - 1:
                        vec.did(ins)
                ins.then_inc(S["v_done"], 1)

            dve.wait_ge(S["ones_ready"], 1)
            for b in range(NB):
                k_rest(b)
                values(b)
                k_low(b)
                if b:
                    metric(b - 1)
            k_max(0)
            queries(0)
            k_max(1)
            queries_rest(0)
            k_max(2)
            queries_low(0)
            k_max(3)
            dve.wait_ge(S["nk_done"], NB)
            dve.tensor_reduce(kmax[0:H, NB:NB + 1], kmax[0:H, 0:NB], AX.X, ALU.max).then_inc(S["kmax_ready"], 1)
            queries(1)
            queries(2)
            queries_rest(1)
            metric(3)
            queries(3)
            shift(0)
            queries_rest(2)
            queries_low(1)
            queries_rest(3)
            queries_low(2)
            queries_low(3)
            for b in range(1, NB):
                shift(b)
            dve.wait_ge(S["ffn_in"], 16 * 3)
            dve.tensor_scalar(wg_f[:, :], wg_i, FFN_SCALE, None, ALU.mult).then_inc(S["ffn_ready"], 1)
            dve.tensor_scalar(wu_f[:, :], wu_i, FFN_SCALE, None, ALU.mult).then_inc(S["ffn_ready"], 1)
            dve.tensor_scalar(wd_f[:, :, :].rearrange("p a b -> p (a b)"), wd_i, FFN_SCALE, 0.5, ALU.mult, ALU.mult)\
                .then_inc(S["ffn_ready"], 1)

            def evacuate(Bk, g):
                dve.wait_ge(S["pv_done"], Bk * NG + g + 1)
                dve.tensor_copy(O_sb[:, g, :], O_bank).then_inc(S["o_evac"], 1)

            TAIL_STEPS, MORE = 30, TPB

            class Tail:
                def __init__(self, Bk, b, p):
                    self.Bk, self.b, self.p = Bk, b, p
                    self.c = Chain(dve, S["tail"], Bk * TAIL_STEPS + MORE * p)

                def normalise(self, placed=False):
                    Bk, c = self.Bk, self.c
                    for g in range(NG - 1):
                        dve.wait_ge(o_in[g], 16 * 2 * GH * (Bk + 1))
                    if placed:
                        c.did(dve.tensor_scalar(rec_T[0:96, :], den_T[0:96, :], SUM_FLOOR, None, ALU.max))
                        dve.wait_ge(S["den_in"], self.p + 1)
                        c.did(dve.tensor_scalar(rec_T[96:128, :], den_T[96:128, :], SUM_FLOOR, None, ALU.max))
                    else:
                        dve.wait_ge(o_in[NG - 1], 16 * 2 * GH * (Bk + 1 - self.p))
                        c.did(dve.tensor_scalar(rec_T, den_T, SUM_FLOOR, None, ALU.max))
                    c.after()
                    c.did(dve.reciprocal(rec_T, rec_T))
                    c.after()
                    if placed:
                        dve.wait_ge(S["num_in"], self.p + 1)
                    dve.tensor_tensor(att_T, num_T, rec_T, ALU.mult).then_inc(S["norm"], 1)

                def checks(self):
                    c = self.c
                    for i, (of, at_, how) in enumerate(((den_T, SUM_FLOOR, ALU.is_ge), (num_T, BIG, ALU.is_le),
                                                        (num_T, -BIG, ALU.is_ge))):
                        c.did(dve.tensor_scalar(junk, of, at_, None, how, ALU.min, accum_out=ok[:, 1, i:i + 1]))
                        c.after()
                    c.did(dve.tensor_tensor(ok[:, 0, 0:3], ok[:, 0, 0:3], ok[:, 1, 0:3], ALU.min))

                def residual(self):
                    Bk, c = self.Bk, self.c
                    r4 = slice(0, TPB)
                    x0, arg, rs, var = (small[:, i, r4] for i in (1, 2, 3, 4))
                    flat = sp1.rearrange("p a b -> p (a b)")
                    dve.wait_ge(S["wo_ps"], Bk + 1)
                    c.did(dve.tensor_scalar(flat, M_bank, 0.1, 8.0, ALU.mult, ALU.min))
                    c.after()
                    c.did(dve.tensor_scalar(flat, flat, -8.0, None, ALU.max))
                    c.after()
                    for t in range(TPB):
                        c.did(dve.tensor_tensor_reduce(sq1[:, t, 1:D], sp1[:, t, 1:D], sp1[:, t, 1:D], 1.0, 0.0,
                                                       ALU.mult, ALU.add, var[:, t:t + 1]))
                    c.after()
                    dve.tensor_scalar(arg, var, 1.0, EPS, ALU.add, ALU.add).then_inc(S["epow_in"], 1)
                    dve.wait_ge(S["epow_out"], 2 * Bk + 1)
                    c.did(dve.tensor_copy(sp1[:, :, 0], x0))
                    c.after()
                    c.did(dve.tensor_tensor(x1, sp1, row3(2, TPB), ALU.mult))
                    c.after()
                    c.did(dve.tensor_tensor(x1, x1, x_tm[:, bass.ds(TPB * self.b, TPB), :], ALU.add))
                    c.after()
                    for t in range(TPB):
                        c.did(dve.bn_stats(stat[:, t, :], x1[:, t, :]))
                    c.after()
                    c.did(dve.tensor_copy(junk[:, 0:1], stat[:, 0, 0:1]))
                    for t in range(TPB):
                        c.did(dve.bn_aggr(mv[:, t, :], stat[:, t, :]))
                    c.after()
                    dve.tensor_scalar(var, mv[:, r4, 1], LN_EPS, None, ALU.add).then_inc(S["epow_in"], 1)
                    dve.wait_ge(S["epow_out"], 2 * Bk + 2)
                    for t in range(TPB):
                        c.did(dve.tensor_scalar(h2[:, t, :], x1[:, t, :], mv[:, t, 0:1], rs[:, t:t + 1],
                                                ALU.subtract, ALU.mult))
                    c.after()
                    c.did(dve.tensor_tensor(h2, h2, row3(4, TPB), ALU.mult))
                    c.after()
                    dve.tensor_tensor(h2, h2, row3(3, TPB), ALU.add).then_inc(S["h2_done"], 1)

                def gated(self, m, gates):
                    n = self.Bk * NM + m
                    dve.wait_ge(S["gate_th"], n + 1)
                    dve.scalar_tensor_tensor(gl[m], th[m], 1.0, gates, ALU.add, ALU.mult).then_inc(S["gated"], 1)

                def glu(self, m, ups):
                    n = self.Bk * NM + m
                    dve.wait_ge(S["gated"], n + 1)
                    dve.wait_ge(S["up_ps"], n + 1)
                    dve.tensor_tensor(hid[:, m, :], ups, gl[m], ALU.mult).then_inc(S["glu_done"], 1)

                def result(self, placed=False):
                    Bk, c = self.Bk, self.c
                    dve.wait_ge(S["down_ps"], Bk + 1)
                    dve.wait_ge(S["y_stored"], 16 * Bk + 1)
                    if placed:
                        for t in range(TPB):
                            c.did(dve.tensor_tensor(y[:, t, :], bank(DOWN_BANK[t])[:, P * t:P * (t + 1)],
                                                    mod[:, 5 * D:6 * D], ALU.mult))
                    else:
                        c.did(dve.tensor_tensor(y, M_bank.rearrange("p (a b) -> p a b", a=TPB), row3(5, TPB),
                                                ALU.mult))
                    c.after()
                    dve.tensor_tensor(y, y, x1, ALU.add).then_inc(S["y_ready"], 1)
                    assert c.n == TAIL_STEPS + (MORE if placed else 0), c.n

            def blocks(p):
                for g in range(NG - 1):
                    evacuate(NB * p, g)
                if p == 0:
                    for b in range(NB):
                        dve.wait_ge(q_st[b], 16)
                with dve.Fori(NB * p + 1, NB * (p + 1)) as Bk:
                    evacuate(Bk - 1, NG - 1)
                    tail = Tail(Bk - 1, Bk - 1 - NB * p, p)
                    tail.normalise()
                    tail.residual()
                    tail.checks()
                    evacuate(Bk, 0)
                    for m in range(NM):
                        tail.gated(m, M_bank)
                        tail.glu(m, M_bank)
                    evacuate(Bk, 1)
                    tail.result()
                    evacuate(Bk, 2)
                last = NB * (p + 1) - 1
                evacuate(last, NG - 1)
                tail = Tail(last, NB - 1, p)
                tail.normalise(placed=True)
                tail.residual()
                tail.checks()
                if p == 0:
                    tail.c.after()
                    dve.tensor_reduce(flag_f[:, 0:1], ok[:, 0, 0:3], AX.X, ALU.min).then_inc(S["flag_in"], 1)
                for m in range(NM):
                    tail.gated(m, bank(m))
                    tail.glu(m, bank(3 + m))
                tail.result(placed=True)
                if p == 0:
                    dve.wait_ge(S["flag_ps"], 1)
                    dve.tensor_scalar(flag_i[0:1, 0:1], bank(2)[0:1, 0:1], P - 0.5, None, ALU.is_lt)\
                        .then_inc(S["flag_ready"], 1)

            dve.memset(mx[:, :, :], 0.0).then_inc(S["max_taken"], 1)
            vec.after()
            dve.tensor_copy(flag_f[:, 2:3], flag_f[:, 1:2]).then_inc(S["y_stored"], 1)
            blocks(0)

            dve.wait_ge(S["flag_ready"], 1)
            with dve.If(dve.value_load(flag_i[0:1, 0:1], min_val=0, max_val=1)):
                MAX_STEPS = 4
                with dve.Fori(0, NB) as b:
                    for h in range(H):
                        for t in range(TPB):
                            dve.wait_ge(S["max_scores"], b * (H * TPB) + h * TPB + t + 1)
                            dve.tensor_reduce(mx[:, t, h:h + 1], ps[:, 0:NB, :], AX.XY, ALU.max)\
                                .then_inc(S["max_taken"], 1)
                    c = Chain(dve, S["vec"], b * MAX_STEPS + vec.n)
                    dve.wait_ge(S["max_T"], b + 1)
                    c.did(dve.tensor_scalar(shift_f[0], M_bank[0:H, :], -1.0, None, ALU.mult))
                    split_shift(c, shift_f[0], shift_parts)
                    assert c.n == MAX_STEPS
                    dve.wait_ge(S["shift_saved"], 16 * (b + 1))
                blocks(1)


_NAMES = ["x", "columns", "wmod", "fixed", "w1t", "w2t", "w_att", "wgt", "wut", "wdt"]


def kernel(**inputs):
    import concourse.bacc as _bacc
    from concourse.bass_utils import run_bass_kernel_spmd as _run

    a = {k: np.asarray(v) for k, v in inputs.items()}
    eta = np.ones((D, 1), np.float32)
    eta[0] = -1.0
    mu = np.zeros((D, 1), np.float32)
    mu[0] = 1.0
    heads = np.repeat(np.eye(H, dtype=np.float32), DH, axis=0)
    lay = {
        "x": a["L0_attn_x"][0],
        "columns": np.concatenate([a["L0_attn_b1"].reshape(MH, P).T, a["L0_attn_b2"].reshape(D, 1), eta, -mu,
                                   a["L0_c"].reshape(D, 1)], axis=1),
        "wmod": a["L0_wmod"],
        "fixed": np.concatenate([np.eye(P, dtype=np.float32), heads] +
                                [np.eye(P, dtype=np.float32)[:, 32 * j + o:32 * j + o + DH]
                                 for o in (0, DH) for j in range(GH)], axis=1),
        "w1t": a["L0_attn_W1"].T,
        "w2t": a["L0_attn_W2"].T.reshape(MH, P, D).transpose(1, 0, 2),
        "w_att": np.stack([a["L0_attn_" + n].T for n in ("Wk", "Wv", "Wq", "Wo")], axis=1),
        "wgt": a["L0_ffn_w_gate"].T, "wut": a["L0_ffn_w_up"].T,
        "wdt": a["L0_ffn_w_down"].T.reshape(NM, P, D).transpose(1, 0, 2).reshape(P, NM * D),
    }
    nc = _bacc.Bacc("TRN2", target_bir_lowering=False, num_devices=1)
    arrays, args = {}, []
    for name in _NAMES:
        v = np.ascontiguousarray(lay[name])
        arrays[f"{name}_dram"] = v
        args.append(nc.dram_tensor(f"{name}_dram", v.shape, mybir.dt.from_np(v.dtype), kind="ExternalInput").ap())
    out = nc.dram_tensor("out_dram", (T, D), F32, kind="ExternalOutput").ap()
    build(nc, *args, out)
    r = _run(nc, [arrays], core_ids=[0])
    return r.results[0]["out_dram"].reshape(1, T, D)
```
